# Optimizing a Trainium2 kernel written in Bass

```python
import numpy as np
import jax
import jax.numpy as jnp

def _softmax(x, axis=-1):
    return jax.nn.softmax(x, axis=axis)

def _gelu(x):
    return jax.nn.gelu(x, approximate=True)

def _silu(x):
    return jax.nn.silu(x)

def _sigmoid(x):
    return jax.nn.sigmoid(x)

def _layernorm(x, axis=-1, eps=1e-05):
    m = jnp.mean(x, axis=axis, keepdims=True)
    v = jnp.var(x, axis=axis, keepdims=True)
    return (x - m) / jnp.sqrt(v + eps)

def _scatter_add(tgt, idx, src, axis=0):
    return tgt.at[idx].add(src)

def _segment_sum(src, seg, n):
    return jax.ops.segment_sum(src, seg, n)
kernel_name = 'mk_vit_tower_d1_tok_img1024_r4_c922ec'

def setup_inputs(seed: int=0):
    np.random.seed(seed)
    _w = jnp.asarray

    def _rec_inputs():
        import jax
        import jax.numpy as jnp
        _rk = jax.random.key(seed)
        x = -0.00016672 + 0.999947 * jax.random.normal(jax.random.fold_in(_rk, 1), (64, 3, 96, 96), jnp.float32)
        return x
    x = _rec_inputs()

    def _L0_tok_setup():
        import jax, jax.numpy as jnp
        import numpy as np
        IMG = 96
        P = 16
        C = 3
        D = 256
        B = 64
        key = jax.random.key(seed)
        kx, kw, kb = jax.random.split(key, 3)
        fan_in = C * P * P
        bound = 1.0 / np.sqrt(fan_in)
        x = jax.random.normal(kx, (B, C, IMG, IMG), dtype=jnp.float32)
        W = jax.random.uniform(kw, (D, fan_in), dtype=jnp.float32, minval=-bound, maxval=bound)
        b = jax.random.uniform(kb, (D,), dtype=jnp.float32, minval=-bound, maxval=bound)
        return {'x': x, 'W': W, 'b': b}
    _L0_tok_all = _L0_tok_setup()
    _L0_tok_in = {k: v for k, v in _L0_tok_all.items() if k in ('W', 'b')}
    del _L0_tok_all

    def _L0_attn_setup():
        import jax, jax.numpy as jnp
        import numpy as np
        import math
        B, T, D = (2, 512, 256)
        N_HEADS = 16
        D_HEAD = D // N_HEADS

        def _rope_tables(t, d_head, dtype=jnp.float32):
            theta = 1.0 / 10000.0 ** (jnp.arange(0, d_head, 2, dtype=jnp.float32) / d_head)
            angles = jnp.outer(jnp.arange(t, dtype=jnp.float32), theta)
            angles = jnp.concatenate([angles, angles], axis=-1)
            return (jnp.cos(angles).astype(dtype), jnp.sin(angles).astype(dtype))

        def _rotate_half(x):
            half = x.shape[-1] // 2
            return jnp.concatenate([-x[..., half:], x[..., :half]], axis=-1)

        def _apply_rope(x, cos, sin):
            return x * cos[None, None] + _rotate_half(x) * sin[None, None]
        key = jax.random.key(seed)
        k1, k2, k3, k4 = jax.random.split(key, 4)
        s_in = 1.0 / math.sqrt(D)
        return {'x': jax.random.normal(k1, (B, T, D), dtype=jnp.float32), 'w_qkv': jax.random.normal(k2, (D, 3 * D), dtype=jnp.float32) * s_in, 'w_out': jax.random.normal(k3, (D, D), dtype=jnp.float32) * s_in, 'b_out': jax.random.normal(k4, (D,), dtype=jnp.float32) * 0.01}
    _L0_attn_all = _L0_attn_setup()
    _L0_attn_in = {k: v for k, v in _L0_attn_all.items() if k in ('w_qkv', 'w_out', 'b_out')}
    del _L0_attn_all

    def _L0_ffn_setup():
        import jax, jax.numpy as jnp
        import numpy as np
        H = 16
        TOP_K = 2
        LN_EPS = 1e-05
        key = jax.random.key(seed)
        ks = jax.random.split(key, 8)
        B, S, E, NE = (2, 256, 256, 8)
        w = lambda k, shp: jax.random.normal(k, shp, dtype=jnp.float32) * 0.02
        return {'x': jax.random.normal(ks[0], (B, S, E), dtype=jnp.float32), 'rW1': w(ks[1], (E // 2, E)), 'rb1': jnp.zeros((E // 2,), jnp.float32), 'ln_g': jnp.ones((E // 2,), jnp.float32), 'ln_b': jnp.zeros((E // 2,), jnp.float32), 'rW2': w(ks[2], (NE, E // 2)), 'rb2': jnp.zeros((NE,), jnp.float32), 'qW': w(ks[3], (NE, E, E)), 'qb': jnp.zeros((NE, E), jnp.float32), 'kW': w(ks[4], (NE, E, E)), 'kb': jnp.zeros((NE, E), jnp.float32), 'vW': w(ks[5], (NE, E, E)), 'vb': jnp.zeros((NE, E), jnp.float32), 'oW': w(ks[6], (NE, E, E)), 'ob': jnp.zeros((NE, E), jnp.float32)}
    _L0_ffn_all = _L0_ffn_setup()
    _L0_ffn_in = {k: v for k, v in _L0_ffn_all.items() if k in ('rW1', 'rb1', 'ln_g', 'ln_b', 'rW2', 'rb2', 'qW', 'qb', 'kW', 'kb', 'vW', 'vb', 'oW', 'ob')}
    del _L0_ffn_all
    return {'x': x, 'L0_tok_W': _L0_tok_in['W'], 'L0_tok_b': _L0_tok_in['b'], 'L0_attn_w_qkv': _L0_attn_in['w_qkv'], 'L0_attn_w_out': _L0_attn_in['w_out'], 'L0_attn_b_out': _L0_attn_in['b_out'], 'L0_ffn_rW1': _L0_ffn_in['rW1'], 'L0_ffn_rb1': _L0_ffn_in['rb1'], 'L0_ffn_ln_g': _L0_ffn_in['ln_g'], 'L0_ffn_ln_b': _L0_ffn_in['ln_b'], 'L0_ffn_rW2': _L0_ffn_in['rW2'], 'L0_ffn_rb2': _L0_ffn_in['rb2'], 'L0_ffn_qW': _L0_ffn_in['qW'], 'L0_ffn_qb': _L0_ffn_in['qb'], 'L0_ffn_kW': _L0_ffn_in['kW'], 'L0_ffn_kb': _L0_ffn_in['kb'], 'L0_ffn_vW': _L0_ffn_in['vW'], 'L0_ffn_vb': _L0_ffn_in['vb'], 'L0_ffn_oW': _L0_ffn_in['oW'], 'L0_ffn_ob': _L0_ffn_in['ob']}

def reference(x, L0_tok_W, L0_tok_b, L0_attn_w_qkv, L0_attn_w_out, L0_attn_b_out, L0_ffn_rW1, L0_ffn_rb1, L0_ffn_ln_g, L0_ffn_ln_b, L0_ffn_rW2, L0_ffn_rb2, L0_ffn_qW, L0_ffn_qb, L0_ffn_kW, L0_ffn_kb, L0_ffn_vW, L0_ffn_vb, L0_ffn_oW, L0_ffn_ob):
    import jax
    import jax.numpy as jnp

    def _L0_tok_ref(x, W, b):
        import jax, jax.numpy as jnp
        import numpy as np
        IMG = 96
        P = 16
        C = 3
        D = 256
        B = 64
        Bsz, Cc, H, Wd = x.shape
        gh, gw = (H // P, Wd // P)
        patches = x.reshape(Bsz, Cc, gh, P, gw, P).transpose(0, 2, 4, 1, 3, 5)
        patches = patches.reshape(Bsz, gh * gw, Cc * P * P)
        return jnp.einsum('bnf,df->bnd', patches, W) + b

    def _L0_attn_ref(x, w_qkv, w_out, b_out):
        import jax, jax.numpy as jnp
        import numpy as np
        import math
        B, T, D = (2, 512, 256)
        N_HEADS = 16
        D_HEAD = D // N_HEADS

        def _rope_tables(t, d_head, dtype=jnp.float32):
            theta = 1.0 / 10000.0 ** (jnp.arange(0, d_head, 2, dtype=jnp.float32) / d_head)
            angles = jnp.outer(jnp.arange(t, dtype=jnp.float32), theta)
            angles = jnp.concatenate([angles, angles], axis=-1)
            return (jnp.cos(angles).astype(dtype), jnp.sin(angles).astype(dtype))

        def _rotate_half(x):
            half = x.shape[-1] // 2
            return jnp.concatenate([-x[..., half:], x[..., :half]], axis=-1)

        def _apply_rope(x, cos, sin):
            return x * cos[None, None] + _rotate_half(x) * sin[None, None]
        b, t, d = x.shape
        qkv = x @ w_qkv
        qkv = qkv.reshape(b, t, 3, N_HEADS, D_HEAD)
        q = jnp.transpose(qkv[:, :, 0], (0, 2, 1, 3))
        k = jnp.transpose(qkv[:, :, 1], (0, 2, 1, 3))
        v = jnp.transpose(qkv[:, :, 2], (0, 2, 1, 3))
        cos, sin = _rope_tables(t, D_HEAD, x.dtype)
        q = _apply_rope(q, cos, sin)
        k = _apply_rope(k, cos, sin)
        scores = jnp.einsum('bhqd,bhkd->bhqk', q, k) / math.sqrt(D_HEAD)
        probs = jax.nn.softmax(scores, axis=-1)
        out = jnp.einsum('bhqk,bhkd->bhqd', probs, v)
        out = jnp.transpose(out, (0, 2, 1, 3)).reshape(b, t, d)
        return out @ w_out + b_out

    def _L0_ffn_ref(x, rW1, rb1, ln_g, ln_b, rW2, rb2, qW, qb, kW, kb, vW, vb, oW, ob):
        import jax, jax.numpy as jnp
        import numpy as np
        H = 16
        TOP_K = 2
        LN_EPS = 1e-05
        B, S, E = x.shape
        NE = qW.shape[0]
        Dh = E // H
        scale = 1.0 / jnp.sqrt(jnp.asarray(Dh, x.dtype))
        h = x @ rW1.T + rb1
        mu = h.mean(-1, keepdims=True)
        var = ((h - mu) ** 2).mean(-1, keepdims=True)
        h = (h - mu) * jax.lax.rsqrt(var + LN_EPS) * ln_g + ln_b
        h = jax.nn.relu(h)
        logits = h @ rW2.T + rb2
        probs = jax.nn.softmax(logits, axis=-1)
        tp, ti = jax.lax.top_k(probs, TOP_K)
        tp = tp / tp.sum(-1, keepdims=True)
        expert_mask = (jax.nn.one_hot(ti, NE, dtype=probs.dtype) * tp[..., None]).sum(-2)
        gates = jnp.moveaxis(expert_mask, -1, 0)

        def expert_step(acc, params):
            qw, qb_, kw, kb_, vw, vb_, ow, ob_, g = params
            q = (x @ qw.T + qb_).reshape(B, S, H, Dh).transpose(0, 2, 1, 3)
            k = (x @ kw.T + kb_).reshape(B, S, H, Dh).transpose(0, 2, 1, 3)
            v = (x @ vw.T + vb_).reshape(B, S, H, Dh).transpose(0, 2, 1, 3)
            scores = jnp.einsum('bhqd,bhkd->bhqk', q, k) * scale
            p = jax.nn.softmax(scores, axis=-1)
            o = jnp.einsum('bhqk,bhkd->bhqd', p, v)
            o = o.transpose(0, 2, 1, 3).reshape(B, S, E) @ ow.T + ob_
            return (acc + o * g[..., None], None)
        out, _ = jax.lax.scan(expert_step, jnp.zeros_like(x), (qW, qb, kW, kb, vW, vb, oW, ob, gates))
        return out
    h = _L0_tok_ref(x, L0_tok_W, L0_tok_b)
    h = h + _L0_attn_ref(_layernorm(h, axis=-1), L0_attn_w_qkv, L0_attn_w_out, L0_attn_b_out)
    h = h + _L0_ffn_ref(_layernorm(h, axis=-1), L0_ffn_rW1, L0_ffn_rb1, L0_ffn_ln_g, L0_ffn_ln_b, L0_ffn_rW2, L0_ffn_rb2, L0_ffn_qW, L0_ffn_qb, L0_ffn_kW, L0_ffn_kb, L0_ffn_vW, L0_ffn_vb, L0_ffn_oW, L0_ffn_ob)
    return h

_drawn_inputs = setup_inputs


def setup_inputs(seed=0):
    import zlib

    import numpy as np

    out = dict(_drawn_inputs(seed))
    spreads = {'L0_ffn_rb1': (0.0, 0.1),
     'L0_ffn_ln_g': (1.0, 0.2),
     'L0_ffn_ln_b': (0.0, 0.1),
     'L0_ffn_rb2': (0.0, 0.1),
     'L0_ffn_qb': (0.0, 0.8),
     'L0_ffn_kb': (0.0, 0.8),
     'L0_ffn_vb': (0.0, 0.1),
     'L0_ffn_ob': (0.0, 0.1)}
    factors = {'L0_attn_b_out': 3.114, 'L0_ffn_qW': 8.0, 'L0_ffn_kW': 8.0}
    for name, (base, spread) in spreads.items():
        noise = np.random.default_rng([zlib.crc32(name.encode()), seed]).standard_normal(out[name].shape)
        drawn = base * np.exp(spread * noise) if base else spread * noise
        out[name] = jnp.asarray(drawn.astype(out[name].dtype))
    for name, factor in factors.items():
        out[name] = (out[name] * factor).astype(out[name].dtype)
    return out
```

```python
from contextlib import ExitStack

import numpy as np

import concourse.bass as bass
from concourse import mybir

F32 = mybir.dt.float32
BF16 = mybir.dt.bfloat16
U32 = mybir.dt.uint32
ALU = mybir.AluOpType
ACT = mybir.ActivationFunctionType
AX = mybir.AxisListType.X

IMAGES, CHANNELS, SIDE, PATCH = 64, 3, 96, 16
GRID = SIDE // PATCH
T = GRID * GRID
D = 256
HEADS, HD = 16, 16
NE = 8
RH = 128
P = 128
KC = D // P
BATCH = 16
NB = IMAGES // BATCH
PAIRS = BATCH // 2
HALF = PAIRS * T
TOK = BATCH * T
HG, HH = 4, 4
HT = HH * T
SLOT = 64
PAD = SLOT - T
STEPS = 1 + NE
FC = CHANNELS * PATCH * PATCH // P
RT = 96
NT = TOK // RT
EPS = 1e-5
NG = 16

CONSTS = {}
_at = 0
for _n, _w in (("ident", P), ("negdiag", T), ("hmask", HH), ("ones_pair", 32), ("mean_d", P), ("mean_r", P),
               ("same_image", P), ("pick_image", P), ("cos", T), ("sin", T), ("iota", NT * NE), ("ones", P), ("eps", 1)):
    CONSTS[_n] = (_at, _at + _w)
    _at += _w
CW = _at


def constants():
    t = np.zeros((P, CW), np.float32)
    row = np.arange(P)

    def put(name, a):
        lo, hi = CONSTS[name]
        t[:, lo:hi] = a

    put("ident", np.eye(P))
    put("negdiag", -(row[:, None] % SLOT == np.arange(T)[None]).astype(np.float32))
    put("hmask", (row[:, None] % SLOT) // HD == np.arange(HH)[None])
    valid = row % SLOT < T
    put("ones_pair", valid[:, None] & (row[:, None] // SLOT == np.arange(32)[None] % 2))
    put("mean_d", 1.0 / D)
    put("mean_r", 1.0 / RH)
    put("same_image", valid[:, None] & valid[None] & (row[:, None] // SLOT == row[None] // SLOT))
    put("pick_image", row[:, None] == row[None] % 2)
    theta = (1.0 / np.float32(10000.0) ** (np.arange(0, HD, 2, dtype=np.float32) / np.float32(HD))).astype(np.float32)
    angle = np.outer(np.arange(T, dtype=np.float32), theta).astype(np.float32)
    angle = np.concatenate([angle, angle], axis=-1)[:, row % HD].T
    put("cos", np.cos(angle))
    put("sin", np.sin(angle) * np.where(row % HD < HD // 2, -1, 1)[:, None])
    put("iota", np.tile(np.arange(NE), NT)[None])
    put("ones", 1.0)
    put("eps", EPS)
    return t


def build(nc, pixels, tokW, tokB, wqkv1, wrot1, wout1, bout1, rW1, rvecs, rW2, rb2, wts, qkb, vb, ob, table, out):
    with ExitStack() as ctx:
        def sb(name, shape, dt=F32):
            return ctx.enter_context(nc.sbuf_tensor(name, shape, dt))

        def sem(name):
            return ctx.enter_context(nc.semaphore(name))

        gate_dram = nc.dram_tensor("gate_dram", (NE, TOK), F32).ap()

        ct = sb("ct", [P, CW])

        def const(name, rows=P):
            lo, hi = CONSTS[name]
            return ct[0:rows, lo:hi]

        same_image = sb("same_image", [P, P], BF16)
        tokw = sb("tokw", [P, FC, D])
        tokb = sb("tokb", [P, KC])
        w1qkv = sb("w1qkv", [P, KC, 3 * D])
        w1rot = sb("w1rot", [P, KC, 2 * D])
        w1out = sb("w1out", [P, KC, D])
        b1out = sb("b1out", [P, KC])
        rw1 = sb("rw1", [P, KC, RH])
        rw2 = sb("rw2", [RH, NE])
        rb2_row = sb("rb2_row", [1, NE])
        rvec = sb("rvec", [RH, 3])
        bias_all = sb("bias_all", [P, NE, 24])
        bias_cur = sb("bias_cur", [P, 24])
        bias_none = sb("bias_none", [P, 24])
        vbias = sb("vbias", [P, D])
        obias = sb("obias", [NE, D])
        wqk = sb("wqk", [P, 2, KC, D])
        wv = sb("wv", [P, KC, D])
        wo = sb("wo", [P, KC, D])

        xpix = sb("xpix", [P, FC, TOK])
        h = sb("h", [P, KC, TOK])
        xn = sb("xn", [P, KC, TOK])
        sq = sb("sq", [P, KC, TOK])
        std = sb("std", [P, 2, HALF])
        rstd = sb("rstd", [P, 2, HALF])
        QH = sb("QH", [P, HG, PAIRS, HT])
        KP = sb("KP", [P, HG, PAIRS, P])
        KH = sb("KH", [P, HG, PAIRS, HT], BF16)
        QP = sb("QP", [P, HG, PAIRS, P], BF16)
        Kb = sb("Kb", [P, HALF], BF16)
        rope_a = sb("rope_a", [P, 2, HALF])
        rope_b = sb("rope_b", [P, 2, HALF])
        rope_q = sb("rope_q", [P, HALF])
        rope_k = sb("rope_k", [P, HALF])
        VP = sb("VP", [P, PAIRS, HEADS, HD, 2])
        rowmax = sb("rowmax", [P, 3, HEADS])
        maxdiag = sb("maxdiag", [P, 3, HEADS, T], BF16)
        probs = sb("probs", [P, 2, HEADS, T])
        rsum = sb("rsum", [P, 2, HH, T])
        scale_o = sb("scale_o", [P, 2, HH, T])
        gate_rep = sb("gate_rep", [P, PAIRS, T])
        ON = sb("ON", [P, HH, PAIRS, T])
        OT = sb("OT", [P, KC, TOK])

        r, rsq = sq[:, 0], sq[:, 1]
        lg = sb("lg", [RT, 4, NT, NE])
        rs = sb("rs", [RT, 4, NT])
        top = sb("top", [RT, NT, 8])
        topi = sb("topi", [RT, NT, 8], U32)
        spare = sb("spare", [RT, 1])
        topf = sb("topf", [RT, NT, 8])
        gsel = sb("gsel", [RT, 2, NT, NE])
        gates = sb("gates", [RT, NT, NE])
        gatesT = sb("gatesT", [NE, TOK])
        gate2 = sb("gate2", [2, NE, HALF])
        hout = sb("hout", [P, KC, TOK])

        bank = [ctx.enter_context(nc.psum_tensor(f"bank{i}", [P, 512], F32)) for i in range(8)]
        proj, maxb, scb, ob_ = bank[0:2], bank[2:4], bank[4:6], bank[6:8]

        S = {n: sem(n) for n in (
            "small_loaded cast_done zeroed bias_masked "
            "x_loaded patch_done h_ready mean_done centered squared var_done std_ready rstd_ready normed "
            "bias_ready q_done q_free k_done k_free rope_part rope_ready kb_ready k_prep "
            "v_done v_free gate_mm gate_ready "
            "max_mm max_ready maxdiag_ready score_done exp_done pv_done rsum_ready scale_ready o_ready "
            "ot_loaded out_done out_added wqk_loaded wv_loaded vbias_loaded wo_loaded "
            "r_done r_ready rmean_done rcentered rsquared rvar_done rstd_done rrstd r_normed r_relu logit_done gstep gexp gates_ready "
            "gtr_done gtr_copied gate_stored gate2_loaded obias_done obias_added hout_ready out_stored").split()}

        block = ctx.enter_context(nc.Block())

        @block.sync
        def _(sp):
            for dst, src in ((ct, table), (tokw, tokW), (tokb, tokB), (w1qkv, wqkv1), (w1rot, wrot1), (w1out, wout1), (b1out, bout1),
                             (rw1, rW1), (rvec, rvecs), (rw2, rW2), (rb2_row, rb2), (bias_all[:, :, 16:24], qkb), (obias, ob)):
                sp.dma_start(dst if dst.__class__.__name__ == "AP" else dst[:], src).then_inc(S["small_loaded"], 16)

            def regroup(s):
                sp.wait_ge(S["o_ready"], s * PAIRS + PAIRS)
                sp.wait_ge(S["out_done"], s * 4)
                for i in range(2):
                    for x_ in range(2):
                        src = ON[i:i + 127:2].rearrange("p (c x) n t -> p x c (n t)", x=2)[:, x_]
                        sp.dma_start(OT[x_ * 64:(x_ + 1) * 64, :, i * HALF:(i + 1) * HALF], src).then_inc(S["ot_loaded"], 16)

            def load_w(e, what):
                src = wts[bass.ds(e, 1)].rearrange("o p t c n -> p (o t) c n")
                if "qk" in what:
                    sp.dma_start(wqk[:], src[:, 0:2]).then_inc(S["wqk_loaded"], 16)
                if "v" in what:
                    sp.dma_start(wv[:], src[:, 2]).then_inc(S["wv_loaded"], 16)
                    sp.dma_start(vbias[:], vb[bass.ds(e, 1)].partition_broadcast(P)).then_inc(S["vbias_loaded"], 16)
                if "o" in what:
                    sp.dma_start(wo[:], src[:, 3]).then_inc(S["wo_loaded"], 16)

            with sp.Fori(0, NB) as b:
                sp.wait_ge(S["patch_done"], b * 4)
                sp.dma_start(xpix[:], pixels[bass.ds(b, 1)].rearrange("o p c n -> p (o c) n")).then_inc(S["x_loaded"], 16)
                s0 = b * STEPS
                sp.wait_ge(S["out_done"], s0 * 4)
                load_w(0, "qk v o")
                regroup(s0)
                sp.wait_ge(S["gtr_copied"], b * 2 + 2)
                sp.dma_start(gate_dram, gatesT[:]).then_inc(S["gate_stored"], 16)
                sp.wait_ge(S["gate_stored"], b * 16 + 16)
                sp.dma_start(gate2[:], gate_dram.rearrange("e (i n) -> i e n", i=2)).then_inc(S["gate2_loaded"], 16)

                def after(s, e, last=False):
                    if not last:
                        sp.wait_ge(S["q_done"], s * HG + HG)
                        sp.wait_ge(S["k_done"], s * HG + HG)
                        load_w(e + 1, "qk")
                        sp.wait_ge(S["v_free"], s * PAIRS + PAIRS)
                        load_w(e + 1, "v")
                    regroup(s)

                after(s0 + 1, 0)
                with sp.Fori(1, NE - 1) as e:
                    s = s0 + 1 + e
                    sp.wait_ge(S["out_done"], s * 4)
                    load_w(e, "o")
                    after(s, e)
                s = s0 + NE
                sp.wait_ge(S["out_done"], s * 4)
                load_w(NE - 1, "o")
                after(s, NE - 1, last=True)
                sp.wait_ge(S["hout_ready"], b + 1)
                sp.dma_start(out[bass.ds(b, 1)].rearrange("o p c n -> p (o c) n"), hout[:]).then_inc(S["out_stored"], 16)
            sp.wait_ge(S["out_stored"], NB * 16)

        @block.tensor
        def _(pe):
            mm = nc.tensor.matmul
            ident = const("ident")

            pe.wait_ge(S["small_loaded"], 13 * 16)
            pe.wait_ge(S["cast_done"], 1)

            def qkv(s, first=False):
                if not first:
                    pe.wait_ge(S["wqk_loaded"], expert_n * 16 + 16)
                for g in range(HG):
                    for t, (ready, free) in enumerate((("q_done", "q_free"), ("k_done", "k_free"))):
                        if g:
                            pe.wait_ge(S[free], s * HG + g)
                        for i in range(2):
                            for c in range(KC):
                                lhsT = w1qkv[:, c, t * D + g * 64:t * D + g * 64 + 64] if first else wqk[:, t, c, g * 64:(g + 1) * 64]
                                last = mm(proj[t][i * 64:(i + 1) * 64, 0:HALF], lhsT, xn[:, c, i * HALF:(i + 1) * HALF],
                                          start=(c == 0), stop=(c == KC - 1))
                        if first:
                            for i in range(2):
                                for c in range(KC):
                                    last = mm(maxb[t][i * 64:(i + 1) * 64, 0:HALF],
                                              w1rot[:, c, t * D + g * 64:t * D + g * 64 + 64],
                                              xn[:, c, i * HALF:(i + 1) * HALF], start=(c == 0), stop=(c == KC - 1))
                        last.then_inc(S[ready], 1)
                if not first:
                    pe.wait_ge(S["wv_loaded"], expert_n * 16 + 16)
                for p in range(PAIRS):
                    if p == 0:
                        pe.wait_ge(S["q_free"], s * HG + HG)
                    elif p == 1:
                        pe.wait_ge(S["k_free"], s * HG + HG)
                    else:
                        pe.wait_ge(S["v_free"], s * PAIRS + p - 1)
                    for i in range(2):
                        at = i * HALF + p * T
                        for c in range(KC):
                            last = mm(proj[p % 2][i * SLOT:i * SLOT + T, 0:D], xn[:, c, at:at + T],
                                      w1qkv[:, c, 2 * D:3 * D] if first else wv[:, c, :], start=(c == 0), stop=(c == KC - 1))
                    last.then_inc(S["v_done"], 1)

            def out_proj(s, w):
                pe.wait_ge(S["ot_loaded"], s * 64 + 64)
                for j in range(4):
                    m, i = j // 2, j % 2
                    if j >= 2:
                        pe.wait_ge(S["out_added"], s * 4 + j - 1)
                    for c in range(KC):
                        last = mm(proj[(j + 1) % 2][:, 0:HALF], w[:, c, m * P:(m + 1) * P],
                                  OT[:, c, i * HALF:(i + 1) * HALF], start=(c == 0), stop=(c == KC - 1))
                    last.then_inc(S["out_done"], 1)

            def gate_product(s, b, e):
                pe.wait_ge(S["v_free"], s * PAIRS + PAIRS - 1)
                if isinstance(e, int) and e == 0:
                    pe.wait_ge(S["gate2_loaded"], b * 16 + 16)
                rhs = gate2[:, e, :] if isinstance(e, int) else gate2[:, bass.ds(e, 1), :].rearrange("i o n -> i (o n)")
                mm(proj[0][:, 0:HALF], const("pick_image", 2), rhs, start=True, stop=True).then_inc(S["gate_mm"], 1)

            def attend(s):
                def maxima(p):
                    for u in range(2):
                        if p:
                            pe.wait_ge(S["max_ready"], s * 16 + 2 * p - 1 + u)
                        for k in range(2):
                            g = 2 * u + k
                            last = mm(maxb[u][:, k * HT:(k + 1) * HT], QP[:, g, p, :], KH[:, g, p, :], start=True, stop=True)
                        last.then_inc(S["max_mm"], 1)

                def scores(p):
                    pe.wait_ge(S["maxdiag_ready"], s * PAIRS + p + 1)
                    for u in range(2):
                        if p:
                            pe.wait_ge(S["exp_done"], s * 16 + 2 * p - 1 + u)
                        for k in range(2):
                            g = 2 * u + k
                            o = scb[u][:, k * HT:(k + 1) * HT]
                            mm(o, KP[:, g, p, :], QH[:, g, p, :], start=True, stop=False)
                            last = mm(o, same_image[:], maxdiag[:, p % 3, g * HH:(g + 1) * HH, :].rearrange("p h t -> p (h t)"),
                                      start=False, stop=True)
                        last.then_inc(S["score_done"], 1)

                def values(p):
                    pe.wait_ge(S["exp_done"], s * 16 + 2 * p + 2)
                    if p >= 2:
                        pe.wait_ge(S["o_ready"], s * PAIRS + p - 1)
                    o = ob_[p % 2]
                    for hh in range(HH):
                        for g in range(HG):
                            n = g * HH + hh
                            mm(o[g * 32:(g + 1) * 32, hh * T:(hh + 1) * T],
                               VP[:, p, n].rearrange("k d i -> k (d i)"), probs[:, p % 2, n, :], start=True, stop=True)
                    for g in range(HG):
                        last = mm(o[g * 32:(g + 1) * 32, HT:2 * HT], const("ones_pair"),
                                  probs[:, p % 2, g * HH:(g + 1) * HH, :].rearrange("p h t -> p (h t)"), start=True, stop=True)
                    last.then_inc(S["pv_done"], 1)

                pe.wait_ge(S["q_free"], s * HG + HG)
                pe.wait_ge(S["k_prep"], s * HG + HG)
                maxima(0)
                maxima(1)
                for p in range(PAIRS):
                    if p + 2 < PAIRS:
                        maxima(p + 2)
                    scores(p)
                    if p == 0:
                        pe.wait_ge(S["v_free"], s * PAIRS + PAIRS)
                    if p:
                        values(p - 1)
                values(PAIRS - 1)

            def norm(n, src_ready):
                for i in range(2):
                    pe.wait_ge(S[src_ready[0]], src_ready[1] + i if src_ready[2] else src_ready[1])
                    for c in range(KC):
                        last = mm(proj[i][:, 0:HALF], const("mean_d"), h[:, c, i * HALF:(i + 1) * HALF],
                                  start=(c == 0), stop=(c == KC - 1))
                    last.then_inc(S["mean_done"], 1)
                for i in range(2):
                    pe.wait_ge(S["squared"], n * 2 + i + 1)
                    for c in range(KC):
                        last = mm(proj[i][:, 0:HALF], const("mean_d"), sq[:, c, i * HALF:(i + 1) * HALF],
                                  start=(c == 0), stop=(c == KC - 1))
                    last.then_inc(S["var_done"], 1)

            with pe.Fori(0, NB) as b:
                s0 = b * STEPS
                pe.wait_ge(S["x_loaded"], b * 16 + 16)
                for j in range(4):
                    m, i = j // 2, j % 2
                    if j >= 2:
                        pe.wait_ge(S["h_ready"], b * 4 + j - 1)
                    for c in range(FC):
                        last = mm(proj[j % 2][:, 0:HALF], tokw[:, c, m * P:(m + 1) * P], xpix[:, c, i * HALF:(i + 1) * HALF],
                                  start=(c == 0), stop=(c == FC - 1))
                    last.then_inc(S["patch_done"], 1)
                norm(b * 2, ("h_ready", b * 4 + 4, False))
                pe.wait_ge(S["normed"], b * 8 + 4)
                pe.wait_ge(S["zeroed"], 4)
                expert_n = None
                qkv(s0, first=True)
                attend(s0)
                out_proj(s0, w1out)
                norm(b * 2 + 1, ("out_added", s0 * 4 + 4, False))
                pe.wait_ge(S["normed"], b * 8 + 8)
                for i in range(2):
                    for c in range(KC):
                        last = mm(proj[i][:, 0:HALF], rw1[:, c, :], xn[:, c, i * HALF:(i + 1) * HALF], start=(c == 0), stop=(c == KC - 1))
                    last.then_inc(S["r_done"], 1)
                for i in range(2):
                    pe.wait_ge(S["r_ready"], b * 2 + i + 1)
                    mm(proj[i][:, 0:HALF], const("mean_r"), r[:, i * HALF:(i + 1) * HALF], start=True, stop=True).then_inc(S["rmean_done"], 1)
                for i in range(2):
                    pe.wait_ge(S["rsquared"], b * 2 + i + 1)
                    mm(proj[i][:, 0:HALF], const("mean_r"), rsq[:, i * HALF:(i + 1) * HALF], start=True, stop=True).then_inc(S["rvar_done"], 1)
                pe.wait_ge(S["r_relu"], b * 2 + 2)
                for t in range(NT):
                    o = proj[0][0:RT, t * NE:(t + 1) * NE]
                    mm(o, r[:, t * RT:(t + 1) * RT], rw2[:], start=True, stop=False)
                    last = mm(o, const("ones", 1)[:, 0:RT], rb2_row[:], start=False, stop=True)
                last.then_inc(S["logit_done"], 1)
                pe.wait_ge(S["gates_ready"], b + 1)
                for i in range(2):
                    for t in range(3):
                        last = nc.tensor.transpose(proj[i][0:NE, t * RT:(t + 1) * RT], gates[:, i * 3 + t, :], ident[0:RT, 0:RT])
                    last.then_inc(S["gtr_done"], 1)
                for j in range(4):
                    m, i = j // 2, j % 2
                    pe.wait_ge(S["gtr_copied"], b * 2 + 2) if j == 0 else None
                    if j >= 2:
                        pe.wait_ge(S["obias_added"], b * 4 + j - 1)
                    mm(proj[j % 2][:, 0:HALF], obias[:, m * P:(m + 1) * P], gatesT[:, i * HALF:(i + 1) * HALF],
                       start=True, stop=True).then_inc(S["obias_done"], 1)
                pe.wait_ge(S["obias_added"], b * 4 + 4)
                expert_n = b * NE
                qkv(s0 + 1)
                gate_product(s0 + 1, b, 0)
                attend(s0 + 1)
                with pe.Fori(1, NE) as e:
                    s = s0 + 1 + e
                    expert_n = b * NE + e
                    pe.wait_ge(S["gate_ready"], expert_n)
                    qkv(s)
                    gate_product(s, b, e)
                    pe.wait_ge(S["wo_loaded"], expert_n * 16)
                    pe.wait_ge(S["v_free"], s * PAIRS + PAIRS)
                    pe.wait_ge(S["gate_ready"], expert_n + 1)
                    out_proj(s - 1, wo)
                    pe.wait_ge(S["out_added"], s * 4)
                    attend(s)
                pe.wait_ge(S["wo_loaded"], (b * NE + NE) * 16)
                out_proj(s0 + NE, wo)
                pe.wait_ge(S["out_added"], (s0 + NE) * 4 + 4)

        @block.scalar
        def _(act):
            act_f = nc.scalar.activation
            hmask = const("hmask")

            def prepare_q(s, src, bias, ready, val):
                for g in range(HG):
                    act.wait_ge(S[ready], val + g + 1)
                    for hh in range(HH):
                        act_f(QH[:, g, :, hh * T:(hh + 1) * T], src, ACT.Identity,
                              bias=bias[:, g * HH + hh:g * HH + hh + 1], scale=hmask[:, hh:hh + 1])
                    for i in range(2):
                        lo, hi = i * 64, (i + 1) * 64
                        last = act_f(QP[lo:hi, g, :, i * SLOT:i * SLOT + T], src[lo:hi], ACT.Identity,
                                     bias=bias[lo:hi, 16 + g:17 + g], scale=1.0)
                    last.then_inc(S["q_free"], 1)

            def exps(s):
                for p in range(PAIRS):
                    for u in range(2):
                        act.wait_ge(S["score_done"], s * 16 + 2 * p + u + 1)
                        if p >= 2 and u == 0:
                            act.wait_ge(S["pv_done"], s * PAIRS + p - 1)
                        act_f(probs[:, p % 2, u * 8:(u + 1) * 8, :], scb[u][:, 0:2 * HT].rearrange("p (h t) -> p h t", t=T),
                              ACT.Exp, scale=HD ** -0.5).then_inc(S["exp_done"], 1)

            def squares(n):
                for i in range(2):
                    act.wait_ge(S["centered"], (n * 2 + i + 1) * 2)
                    act_f(sq[:, :, i * HALF:(i + 1) * HALF], xn[:, :, i * HALF:(i + 1) * HALF], ACT.Square).then_inc(S["squared"], 1)
                for i in range(2):
                    act.wait_ge(S["var_done"], n * 2 + i + 1)
                    act_f(std[:, i], proj[i][:, 0:HALF], ACT.Sqrt, bias=const("eps"), scale=1.0).then_inc(S["std_ready"], 1)

            act.wait_ge(S["small_loaded"], 13 * 16)
            act.wait_ge(S["zeroed"], 4)
            with act.Fori(0, NB) as b:
                s0 = b * STEPS
                for j in range(4):
                    m, i = j // 2, j % 2
                    act.wait_ge(S["patch_done"], b * 4 + j + 1)
                    act_f(h[:, m, i * HALF:(i + 1) * HALF], proj[j % 2][:, 0:HALF], ACT.Identity, bias=tokb[:, m:m + 1],
                          scale=1.0).then_inc(S["h_ready"], 1)
                squares(b * 2)
                prepare_q(s0, rope_q[:].rearrange("p (n t) -> p n t", t=T), bias_none, "rope_ready", b * HG)
                exps(s0)
                squares(b * 2 + 1)
                for i in range(2):
                    act.wait_ge(S["r_done"], b * 2 + i + 1)
                    act_f(r[:, i * HALF:(i + 1) * HALF], proj[i][:, 0:HALF], ACT.Identity, bias=rvec[:, 0:1], scale=1.0).then_inc(S["r_ready"], 1)
                for i in range(2):
                    act.wait_ge(S["rcentered"], b * 2 + i + 1)
                    act_f(rsq[:, i * HALF:(i + 1) * HALF], r[:, i * HALF:(i + 1) * HALF], ACT.Square).then_inc(S["rsquared"], 1)
                for i in range(2):
                    act.wait_ge(S["rvar_done"], b * 2 + i + 1)
                    act_f(std[:, i], proj[i][:, 0:HALF], ACT.Sqrt, bias=const("eps"), scale=1.0).then_inc(S["rstd_done"], 1)
                for i in range(2):
                    act.wait_ge(S["r_normed"], b * 2 + i + 1)
                    act_f(r[:, i * HALF:(i + 1) * HALF], r[:, i * HALF:(i + 1) * HALF], ACT.Relu, bias=rvec[:, 2:3],
                          scale=rvec[:, 1:2]).then_inc(S["r_relu"], 1)
                act.wait_ge(S["gstep"], b * NG + 2)
                act_f(lg[:, 1], lg[:, 0], ACT.Exp).then_inc(S["gexp"], 1)

                def expert(s, n):
                    act.wait_ge(S["bias_ready"], n + 1)
                    prepare_q(s, proj[0][:, 0:HALF].rearrange("p (n t) -> p n t", t=T), bias_cur, "q_done", s * HG)
                    act.wait_ge(S["gate_mm"], n + 1)
                    act.wait_ge(S["o_ready"], s * PAIRS)
                    act_f(gate_rep[:].rearrange("p n t -> p (n t)"), proj[0][:, 0:HALF], ACT.Copy).then_inc(S["gate_ready"], 1)
                    exps(s)

                expert(s0 + 1, b * NE)
                with act.Fori(1, NE) as e:
                    expert(s0 + 1 + e, b * NE + e)


        @block.vector
        def _(dve):
            v = nc.vector
            hmask = const("hmask")

            v.memset(KP[:], 0.0).then_inc(S["zeroed"], 1)
            v.memset(bias_none[:], 0.0).then_inc(S["zeroed"], 1)
            dve.wait_ge(S["small_loaded"], 13 * 16)
            v.tensor_copy(same_image[:], const("same_image")).then_inc(S["cast_done"], 1)
            for g in range(HG):
                for hh in range(HH):
                    last = v.tensor_scalar(bias_all[:, :, g * HH + hh], bias_all[:, :, 16 + g], hmask[:, hh:hh + 1], None, ALU.mult)
            last.then_inc(S["bias_masked"], 1)

            def prepare_k(s, src, bias, first, bb):
                for g in range(HG):
                    if first:
                        rope(s, g, bb)
                    else:
                        dve.wait_ge(S["k_done"], s * HG + g + 1)
                    for i in range(2):
                        lo, hi = i * 64, (i + 1) * 64
                        v.tensor_scalar(KP[lo:hi, g, :, i * SLOT:i * SLOT + T], src[lo:hi], bias[lo:hi, 20 + g:21 + g], None, ALU.add)
                    dve.wait_ge(S["k_prep"], s * HG + g)
                    last = v.tensor_scalar(Kb[:].rearrange("p (n t) -> p n t", t=T), src, bias[:, 20 + g:21 + g], None, ALU.add)
                    last.then_inc(S["k_free"], 1)
                    dve.wait_ge(S["k_free"], s * HG + g + 1)
                    for hh in range(HH):
                        last = v.tensor_scalar(KH[:, g, :, hh * T:(hh + 1) * T], Kb[:].rearrange("p (n t) -> p n t", t=T),
                                               hmask[:, hh:hh + 1], None, ALU.mult)
                    last.then_inc(S["k_prep"], 1)

            def rope(s, g, bb):
                cos = const("cos").unsqueeze(1).to_broadcast([P, PAIRS, T])
                sin = const("sin").unsqueeze(1).to_broadcast([P, PAIRS, T])
                for t, (done, dst) in enumerate((("q_done", rope_q), ("k_done", rope_k))):
                    dve.wait_ge(S[done], s * HG + g + 1)
                    v.tensor_tensor(rope_a[:, t].rearrange("p (n t) -> p n t", t=T), proj[t][:, 0:HALF].rearrange("p (n t) -> p n t", t=T), cos,
                                    ALU.mult).then_inc(S["rope_part"], 1)
                    v.tensor_tensor(rope_b[:, t].rearrange("p (n t) -> p n t", t=T), maxb[t][:, 0:HALF].rearrange("p (n t) -> p n t", t=T), sin,
                                    ALU.mult).then_inc(S["rope_part"], 1)
                    dve.wait_ge(S["rope_part"], (bb * 8 + g * 2 + t) * 2 + 2)
                    if t == 0 and g:
                        dve.wait_ge(S["q_free"], s * HG + g)
                    v.tensor_tensor(dst[:], rope_a[:, t], rope_b[:, t], ALU.add).then_inc(S["rope_ready"] if t == 0 else S["kb_ready"], 1)
                dve.wait_ge(S["kb_ready"], bb * 4 + g + 1)

            def copy_v(s, n=None):
                if n is not None:
                    dve.wait_ge(S["vbias_loaded"], n * 16 + 16)
                for p in range(PAIRS):
                    dve.wait_ge(S["v_done"], s * PAIRS + p + 1)
                    for i in range(2):
                        rows = slice(i * SLOT, i * SLOT + T)
                        src = proj[p % 2][rows, 0:D].rearrange("k (n d) -> k n d", d=HD)
                        if n is None:
                            last = v.tensor_copy(VP[rows, p, :, :, i], src)
                        else:
                            last = v.tensor_tensor(VP[rows, p, :, :, i], src, vbias[rows].rearrange("k (n d) -> k n d", d=HD), ALU.add)
                    last.then_inc(S["v_free"], 1)

            def add_out(s, bias):
                for j in range(4):
                    m, i = j // 2, j % 2
                    dve.wait_ge(S["out_done"], s * 4 + j + 1)
                    hs = h[:, m, i * HALF:(i + 1) * HALF]
                    if bias is None:
                        v.tensor_tensor(hs, proj[(j + 1) % 2][:, 0:HALF], hs, ALU.add).then_inc(S["out_added"], 1)
                    else:
                        v.scalar_tensor_tensor(out=hs, in0=proj[(j + 1) % 2][:, 0:HALF], scalar=bias[:, m:m + 1], in1=hs,
                                               op0=ALU.add, op1=ALU.add).then_inc(S["out_added"], 1)

            def attend(s, gated, n):
                def maxima(p):
                    if p >= 3:
                        dve.wait_ge(S["maxdiag_ready"], s * PAIRS + p - 2)
                    for u in range(2):
                        dve.wait_ge(S["max_mm"], s * 16 + 2 * p + u + 1)
                        v.tensor_reduce(rowmax[:, p % 3, u * 8:(u + 1) * 8], maxb[u][:, 0:2 * HT].rearrange("p (h t) -> p h t", t=T), AX,
                                        ALU.max).then_inc(S["max_ready"], 1)

                def normalize(p):
                    dve.wait_ge(S["pv_done"], s * PAIRS + p + 1)
                    o = ob_[p % 2]
                    v.reciprocal(rsum[:, p % 2], o[:, HT:2 * HT].rearrange("p (h t) -> p h t", t=T)).then_inc(S["rsum_ready"], 1)
                    if p == 0:
                        dve.wait_ge(S["ot_loaded"], s * 64)
                    dve.wait_ge(S["rsum_ready"], s * PAIRS + p + 1)
                    factor = rsum
                    if gated:
                        if p == 0:
                            dve.wait_ge(S["gate_ready"], n + 1)
                        v.tensor_tensor(scale_o[:, p % 2], rsum[:, p % 2], gate_rep[:, p:p + 1, :].to_broadcast([P, HH, T]),
                                        ALU.mult).then_inc(S["scale_ready"], 1)
                        dve.wait_ge(S["scale_ready"], n * PAIRS + p + 1)
                        factor = scale_o
                    v.tensor_tensor(ON[:, :, p, :], o[:, 0:HT].rearrange("p (h t) -> p h t", t=T), factor[:, p % 2],
                                    ALU.mult).then_inc(S["o_ready"], 1)

                maxima(0)
                maxima(1)
                for p in range(PAIRS):
                    if p + 2 < PAIRS:
                        maxima(p + 2)
                    if p:
                        normalize(p - 1)
                normalize(PAIRS - 1)

            def norm(n):
                for i in range(2):
                    dve.wait_ge(S["mean_done"], n * 2 + i + 1)
                    for c in range(KC):
                        v.tensor_tensor(xn[:, c, i * HALF:(i + 1) * HALF], h[:, c, i * HALF:(i + 1) * HALF], proj[i][:, 0:HALF],
                                        ALU.subtract).then_inc(S["centered"], 1)
                for i in range(2):
                    dve.wait_ge(S["std_ready"], n * 2 + i + 1)
                    v.reciprocal(rstd[:, i], std[:, i]).then_inc(S["rstd_ready"], 1)
                    dve.wait_ge(S["rstd_ready"], n * 2 + i + 1)
                    for c in range(KC):
                        xs = xn[:, c, i * HALF:(i + 1) * HALF]
                        v.tensor_tensor(xs, xs, rstd[:, i], ALU.mult).then_inc(S["normed"], 1)

            def make_gates(b):
                step = [0]

                def then(ins):
                    step[0] += 1
                    ins.then_inc(S["gstep"], 1)
                    dve.wait_ge(S["gstep"], b * NG + step[0])

                wide = lambda a: a.unsqueeze(2).to_broadcast([RT, NT, NE])
                dve.wait_ge(S["logit_done"], b + 1)
                logits = proj[0][0:RT, 0:NT * NE].rearrange("p (t e) -> p t e", e=NE)
                then(v.tensor_reduce(rs[:, 0], logits, AX, ALU.max))
                then(v.tensor_tensor(lg[:, 0], logits, wide(rs[:, 0]), ALU.subtract))
                dve.wait_ge(S["gexp"], b + 1)
                then(v.tensor_reduce(rs[:, 1], lg[:, 1], AX, ALU.add))
                then(v.reciprocal(rs[:, 2], rs[:, 1]))
                then(v.tensor_tensor(lg[:, 2], lg[:, 1], wide(rs[:, 2]), ALU.mult))
                v.memset(spare[:], 0.0)
                for t in range(NT):
                    last = v.max(top[:, t, :], lg[:, 2, t, :])
                then(last)
                v.memset(spare[:], 0.0)
                for t in range(NT):
                    last = v.max_index(topi[:, t, :], top[:, t, :], lg[:, 2, t, :])
                then(last)
                then(v.tensor_copy(topf[:], topi[:]))
                then(v.tensor_tensor(rs[:, 3], top[:, :, 0], top[:, :, 1], ALU.add))
                then(v.reciprocal(rs[:, 0], rs[:, 3]))
                iota = const("iota", RT).rearrange("p (t e) -> p t e", e=NE)
                for k in range(2):
                    then(v.tensor_tensor(gsel[:, k], iota, wide(topf[:, :, k]), ALU.is_equal))
                    then(v.tensor_tensor(gsel[:, k], gsel[:, k], wide(top[:, :, k]), ALU.mult))
                then(v.tensor_tensor(lg[:, 3], gsel[:, 0], gsel[:, 1], ALU.add))
                v.tensor_tensor(gates[:], lg[:, 3], wide(rs[:, 0]), ALU.mult).then_inc(S["gates_ready"], 1)
                then(v.memset(rs[:, 3], 0.0))
                assert step[0] == NG

            with dve.Fori(0, NB) as b:
                s0 = b * STEPS
                norm(b * 2)
                prepare_k(s0, rope_k[:].rearrange("p (n t) -> p n t", t=T), bias_none, True, b)
                copy_v(s0)
                attend(s0, False, None)
                add_out(s0, b1out)
                norm(b * 2 + 1)
                for i in range(2):
                    dve.wait_ge(S["rmean_done"], b * 2 + i + 1)
                    rr = r[:, i * HALF:(i + 1) * HALF]
                    v.tensor_tensor(rr, rr, proj[i][:, 0:HALF], ALU.subtract).then_inc(S["rcentered"], 1)
                for i in range(2):
                    dve.wait_ge(S["rstd_done"], b * 2 + i + 1)
                    v.reciprocal(rstd[:, i], std[:, i]).then_inc(S["rrstd"], 1)
                    dve.wait_ge(S["rrstd"], b * 2 + i + 1)
                    rr = r[:, i * HALF:(i + 1) * HALF]
                    v.tensor_tensor(rr, rr, rstd[:, i], ALU.mult).then_inc(S["r_normed"], 1)
                make_gates(b)
                for i in range(2):
                    dve.wait_ge(S["gtr_done"], b * 2 + i + 1)
                    if i == 0:
                        dve.wait_ge(S["gate_stored"], b * 16)
                    v.tensor_copy(gatesT[:, i * HALF:(i + 1) * HALF], proj[i][0:NE, 0:HALF]).then_inc(S["gtr_copied"], 1)
                for j in range(4):
                    m, i = j // 2, j % 2
                    dve.wait_ge(S["obias_done"], b * 4 + j + 1)
                    hs = h[:, m, i * HALF:(i + 1) * HALF]
                    v.tensor_tensor(hs, proj[j % 2][:, 0:HALF], hs, ALU.add).then_inc(S["obias_added"], 1)

                def expert(s, n, flush):
                    dve.wait_ge(S["bias_ready"], n + 1)
                    prepare_k(s, proj[1][:, 0:HALF].rearrange("p (n t) -> p n t", t=T), bias_cur, False, None)
                    copy_v(s, n)
                    if flush:
                        add_out(s - 1, None)
                    attend(s, True, n)

                expert(s0 + 1, b * NE, False)
                with dve.Fori(1, NE) as e:
                    expert(s0 + 1 + e, b * NE + e, True)
                add_out(s0 + NE, None)
                dve.wait_ge(S["out_stored"], b * 16)
                dve.wait_ge(S["out_added"], (s0 + NE) * 4 + 4)
                v.tensor_copy(hout[:], h[:]).then_inc(S["hout_ready"], 1)

        @block.gpsimd
        def _(pool):
            g_ = nc.gpsimd
            g_.memset(QP[:], 0.0).then_inc(S["zeroed"], 1)
            g_.memset(VP[:], 0.0).then_inc(S["zeroed"], 1)
            pool.wait_ge(S["small_loaded"], 13 * 16)

            def diagonals(s):
                diag = const("negdiag").unsqueeze(1).to_broadcast([P, HEADS, T])
                for p in range(PAIRS):
                    pool.wait_ge(S["max_ready"], s * 16 + 2 * p + 2)
                    if p >= 3:
                        pool.wait_ge(S["score_done"], s * 16 + 2 * (p - 2))
                    g_.tensor_tensor(maxdiag[:, p % 3], rowmax[:, p % 3].unsqueeze(2).to_broadcast([P, HEADS, T]), diag,
                                     ALU.mult).then_inc(S["maxdiag_ready"], 1)

            def biases(s, e, n):
                pool.wait_ge(S["q_free"], s * HG)
                pool.wait_ge(S["k_free"], s * HG)
                g_.tensor_copy(bias_cur[:], bias_all[:, bass.ds(e, 1), :].rearrange("p o n -> p (o n)")).then_inc(S["bias_ready"], 1)

            pool.wait_ge(S["bias_masked"], 1)
            with pool.Fori(0, NB) as b:
                s0 = b * STEPS
                diagonals(s0)
                with pool.Fori(0, NE) as e:
                    biases(s0 + 1 + e, e, b * NE + e)
                    diagonals(s0 + 1 + e)


def rows(a, n=P):
    return a.reshape(-1, n, *a.shape[1:]).swapaxes(0, 1)


def kernel(x, L0_tok_W, L0_tok_b, L0_attn_w_qkv, L0_attn_w_out, L0_attn_b_out, L0_ffn_rW1, L0_ffn_rb1, L0_ffn_ln_g,
           L0_ffn_ln_b, L0_ffn_rW2, L0_ffn_rb2, L0_ffn_qW, L0_ffn_qb, L0_ffn_kW, L0_ffn_kb, L0_ffn_vW, L0_ffn_vb,
           L0_ffn_oW, L0_ffn_ob):
    import concourse.bacc as _bacc
    from concourse.bass_utils import run_bass_kernel_spmd as _run

    pixels = np.asarray(x).reshape(NB, BATCH, CHANNELS, GRID, PATCH, GRID, PATCH).transpose(0, 2, 4, 6, 1, 3, 5)
    pixels = pixels.reshape(NB, FC, P, TOK).swapaxes(1, 2)

    def heads_rows(w):
        return np.asarray(w).reshape(HG, 2, 2, HD, D).transpose(2, 0, 3, 1, 4).reshape(P, KC, D)

    qkv = np.asarray(L0_attn_w_qkv)
    partner = qkv[:, :2 * D].reshape(D, 2 * HEADS, 2, HD // 2)[:, :, ::-1].reshape(D, 2 * D)
    experts = [np.stack([rows(np.asarray(w)[e].T) for w in (L0_ffn_qW, L0_ffn_kW, L0_ffn_vW)]
                        + [heads_rows(np.asarray(L0_ffn_oW)[e].T)], axis=1) for e in range(NE)]
    qkb = np.stack([np.asarray(b).reshape(NE, HG, SLOT) for b in (L0_ffn_qb, L0_ffn_kb)], axis=1)
    qkb = np.concatenate([qkb.transpose(3, 0, 1, 2).reshape(SLOT, NE, 2 * HG)] * 2)
    arrays = {
        "pixels": pixels, "tok_W": rows(np.asarray(L0_tok_W).T), "tok_b": rows(np.asarray(L0_tok_b)),
        "w_qkv": rows(qkv), "w_partner": rows(partner), "w_out": heads_rows(L0_attn_w_out), "b_out": rows(np.asarray(L0_attn_b_out)),
        "rW1": rows(np.asarray(L0_ffn_rW1).T), "rvec": np.stack([np.asarray(a) for a in (L0_ffn_rb1, L0_ffn_ln_g, L0_ffn_ln_b)], axis=1),
        "rW2": np.asarray(L0_ffn_rW2).T, "rb2": np.asarray(L0_ffn_rb2)[None], "experts": np.stack(experts), "qk_bias": qkb,
        "v_bias": np.asarray(L0_ffn_vb), "o_bias": np.asarray(L0_ffn_ob), "table": constants(),
    }
    arrays = {k: np.ascontiguousarray(a) for k, a in arrays.items()}
    nc = _bacc.Bacc("TRN2", target_bir_lowering=False, num_devices=1)
    args = [nc.dram_tensor(f"in_{name}", a.shape, mybir.dt.from_np(a.dtype), kind="ExternalInput").ap()
            for name, a in arrays.items()]
    out = nc.dram_tensor("out_h", (NB, P, KC, TOK), F32, kind="ExternalOutput").ap()
    build(nc, *args, out)
    r = _run(nc, [{f"in_{k}": a for k, a in arrays.items()}], core_ids=[0])
    return r.results[0]["out_h"].transpose(0, 3, 2, 1).reshape(IMAGES, T, D)
```

```python
from contextlib import ExitStack

import numpy as np

import concourse.bass as bass
from concourse import mybir

F32 = mybir.dt.float32
BF16 = mybir.dt.bfloat16
U32 = mybir.dt.uint32
ALU = mybir.AluOpType
ACT = mybir.ActivationFunctionType
AX = mybir.AxisListType.X

IMAGES, CHANNELS, SIDE, PATCH = 64, 3, 96, 16
GRID = SIDE // PATCH
T = GRID * GRID
D = 256
HEADS, HD = 16, 16
NE = 8
RH = 128
P = 128
KC = D // P
BATCH = 16
NB = IMAGES // BATCH
PAIRS = BATCH // 2
HALF = PAIRS * T
TOK = BATCH * T
HG, HH = 4, 4
HT = HH * T
SLOT = 64
PAD = SLOT - T
S2 = NB
FC = CHANNELS * PATCH * PATCH // P
RT = 96
NT = NB * TOK // RT
EPS = 1e-5

CONSTS = {}
_at = 0
for _n, _w in (("ident", P), ("negdiag", T), ("hmask", HH), ("ones_pair", 32), ("mean_d", P), ("mean_r", P),
               ("same_image", P), ("pick_image", P), ("cos", T), ("sin", T), ("iota", NT * NE), ("ones", P), ("eps", 1)):
    CONSTS[_n] = (_at, _at + _w)
    _at += _w
CW = _at


def constants():
    t = np.zeros((P, CW), np.float32)
    row = np.arange(P)

    def put(name, a):
        lo, hi = CONSTS[name]
        t[:, lo:hi] = a

    put("ident", np.eye(P))
    put("negdiag", -(row[:, None] % SLOT == np.arange(T)[None]).astype(np.float32))
    put("hmask", (row[:, None] % SLOT) // HD == np.arange(HH)[None])
    valid = row % SLOT < T
    put("ones_pair", valid[:, None] & (row[:, None] // SLOT == np.arange(32)[None] % 2))
    put("mean_d", 1.0 / D)
    put("mean_r", 1.0 / RH)
    put("same_image", valid[:, None] & valid[None] & (row[:, None] // SLOT == row[None] // SLOT))
    put("pick_image", row[:, None] == row[None] % 2)
    theta = (1.0 / np.float32(10000.0) ** (np.arange(0, HD, 2, dtype=np.float32) / np.float32(HD))).astype(np.float32)
    angle = np.outer(np.arange(T, dtype=np.float32), theta).astype(np.float32)
    angle = np.concatenate([angle, angle], axis=-1)[:, row % HD].T
    put("cos", np.cos(angle))
    put("sin", np.sin(angle) * np.where(row % HD < HD // 2, -1, 1)[:, None])
    put("iota", np.tile(np.arange(NE), NT)[None])
    put("ones", 1.0)
    put("eps", EPS)
    return t


def build(nc, pixels, tokW, tokB, wqkv1, wrot1, wout1, bout1, rW1, rvecs, rW2, rb2, wts, qkb, vb, oW, ob, table, out):
    with ExitStack() as ctx:
        def sb(name, shape, dt=F32):
            return ctx.enter_context(nc.sbuf_tensor(name, shape, dt))

        gate_dram = nc.dram_tensor("gate_dram", (NE, NB, 2, HALF), F32).ap()

        ct = sb("ct", [P, CW])

        def const(name, rows=P):
            lo, hi = CONSTS[name]
            return ct[0:rows, lo:hi]

        same_image = sb("same_image", [P, P], BF16)
        tokb = sb("tokb", [P, KC])
        wrot = sb("wrot", [P, KC, 2 * D])
        wqk = sb("wqk", [P, 2, KC, D])
        wv = sb("wv", [P, KC, D])
        wo = sb("wo", [P, KC, D])
        bout = sb("bout", [P, KC])
        rw1 = sb("rw1", [P, KC, RH])
        rw2 = sb("rw2", [RH, NE])
        rb2_row = sb("rb2_row", [1, NE])
        rvec = sb("rvec", [RH, 3])
        bias_all = sb("bias_all", [P, NE, 24])
        bias_cur = sb("bias_cur", [P, 24])
        bias_none = sb("bias_none", [P, 24])
        vbT = sb("vbT", [P, KC, NE])
        obias_col = sb("obias_col", [P, KC, NE])
        ob_nat = sb("ob_nat", [NE, D])
        obias = sb("obias", [NE, D])

        h = sb("h", [P, NB, KC, TOK])
        xn = sb("xn", [P, NB, KC, TOK])
        sq = sb("sq", [P, KC, TOK])
        std = sb("std", [P, 2, HALF])
        rstd = sb("rstd", [P, 2, HALF])
        QH = sb("QH", [P, 2, HG, PAIRS, HT])
        KP = sb("KP", [P, 2, HG, PAIRS, P])
        KH = sb("KH", [P, 2, HG, PAIRS, HT], BF16)
        QP = sb("QP", [P, 2, HG, PAIRS, P], BF16)
        Kb = sb("Kb", [P, HALF], BF16)
        VP = sb("VP", [P, PAIRS, HEADS, HD, 2])
        rowmax = sb("rowmax", [P, 4, HEADS])
        maxdiag = sb("maxdiag", [P, 4, HEADS, T], BF16)
        probs = sb("probs", [P, 2, HEADS, T])
        rsum = sb("rsum", [P, 2, HH, T])
        scale_o = sb("scale_o", [P, 2, HH, T])
        gate_rep = sb("gate_rep", [P, 2, PAIRS, T])
        ON = sb("ON", [P, HH, PAIRS, T])
        OT = sb("OT", [P, KC, TOK])
        rope_a, rope_b = sq[:, 0].rearrange("p (t n) -> p t n", t=2), sq[:, 1].rearrange("p (t n) -> p t n", t=2)
        rope_q, rope_k = std[:, 0], std[:, 1]

        def room(tile, t, n):
            return tile[:, t].rearrange("p g n t -> p (g n t)")[:, 0:n]

        xpix = [room(QH, t, FC * TOK).rearrange("p (c n) -> p c n", c=FC) for t in range(2)]
        oW_all = room(KP, 0, NE * KC * D).rearrange("p (e c n) -> p e c n", e=NE, c=KC)
        tokw = room(KP, 1, FC * D).rearrange("p (c n) -> p c n", c=FC)
        gatesT = room(QH, 0, NB * TOK)[0:NE]
        r = room(QH, 1, NB * TOK)
        rsq = room(QH, 1, 2 * NB * TOK)[:, NB * TOK:]

        KH_room = KH[0:RT, 1].rearrange("p g n t -> p (g n t)").bitcast(F32)
        _at = [0]

        def small(*shape, dt=F32):
            n = int(np.prod(shape))
            a = KH_room[:, _at[0]:_at[0] + n]
            _at[0] += n
            a = a.bitcast(U32) if dt == U32 else a
            return a if len(shape) == 1 else a.rearrange("p (a b) -> p a b", a=shape[0]) if len(shape) == 2 else \
                a.rearrange("p (a b c) -> p a b c", a=shape[0], b=shape[1])

        lg, rs = small(4, NT, NE), small(4, NT)
        top, topi, topf = small(NT, 8), small(NT, 8, dt=U32), small(NT, 8)
        gsel, gates = small(2, NT, NE), small(NT, NE)

        bank = [ctx.enter_context(nc.psum_tensor(f"bank{i}", [P, 512], F32)) for i in range(8)]
        proj, maxb, scb, valb = bank[0:2], bank[2:4], bank[4:6], bank[6:8]

        S = {n: ctx.enter_context(nc.semaphore(n)) for n in (
            "small_loaded oW_loaded rope_w_loaded cast_done zeroed bias_masked obcol_mm obcol_copied obias_tr obias_made "
            "x_loaded patch_done h_ready mean_done centered squared var_done std_ready rstd_ready normed "
            "bias_ready q_done q_free k_done k_free rope_part rope_q_ready rope_k_ready k_prep "
            "v_done v_free gate_loaded0 gate_loaded1 "
            "max_mm max_ready maxdiag_ready score_done exp_done pv_done rsum_ready scale_ready o_ready "
            "ot_loaded out_done out_added wqk_loaded wv_loaded wo_loaded "
            "r_done r_ready rmean_done rcentered rsquared rvar_done rstd_done rrstd r_normed r_relu logit_done gstep gexp "
            "gates_ready gtr_done gtr_copied gate_stored gobias_done gobias_added out_stored").split()}

        block = ctx.enter_context(nc.Block())
        NSMALL = 10
        half = lambda i: slice(i * HALF, (i + 1) * HALF)
        by_token = lambda a: a.rearrange("p (n t) -> p n t", t=T)

        def step(e, b):
            return S2 + e * NB + b

        @block.sync
        def _(sp):
            def load(dst, src, s):
                sp.dma_start(dst, src).then_inc(S[s], 16)

            load(tokw, tokW, "small_loaded")
            load(xpix[0], pixels[0], "x_loaded")
            for dst, src in ((ct[:], table), (tokb[:], tokB), (rvec[:], rvecs), (rw1[:], rW1), (rw2[:], rW2), (rb2_row[:], rb2),
                             (bias_all[:, :, 16:24], qkb), (vbT[:], vb), (ob_nat[:], ob)):
                load(dst, src, "small_loaded")
            sp.wait_ge(S["x_loaded"], 16)
            load(xpix[1], pixels[1], "x_loaded")
            load(oW_all, oW, "oW_loaded")
            load(wqk[:, 0], wqkv1[:, :, 0:D], "rope_w_loaded")
            load(wqk[:, 1], wqkv1[:, :, D:2 * D], "rope_w_loaded")
            load(wv[:], wqkv1[:, :, 2 * D:3 * D], "rope_w_loaded")
            load(wo[:], wout1, "rope_w_loaded")
            load(wrot[:], wrot1, "rope_w_loaded")
            load(bout[:], bout1, "rope_w_loaded")
            for b in range(2, NB):
                sp.wait_ge(S["x_loaded"], b * 16)
                sp.wait_ge(S["patch_done"], (b - 2) * 4 + 4)
                load(xpix[b % 2], pixels[b], "x_loaded")

            def regroup(s):
                sp.wait_ge(S["o_ready"], s * PAIRS + PAIRS)
                for i in range(2):
                    for x_ in range(2):
                        src = ON[i:i + 127:2].rearrange("p (c x) n t -> p x c (n t)", x=2)[:, x_]
                        load(OT[x_ * 64:(x_ + 1) * 64, :, half(i)], src, "ot_loaded")

            def load_gates(e, b):
                for i in range(2):
                    src = gate_dram[bass.ds(e, 1), b, i] if not isinstance(e, int) else gate_dram[e:e + 1, b, i]
                    load(gate_rep[i:i + 127:2, b % 2].rearrange("p n t -> p (n t)"), src.partition_broadcast(64).rearrange("q o n -> q (o n)"),
                         f"gate_loaded{b % 2}")

            def matrix(e, t):
                if isinstance(e, int):
                    return wts[e, :, t]
                return wts[bass.ds(e, 1)].rearrange("o p t c n -> p (o t) c n")[:, t]

            for b in range(NB):
                regroup(b)
            load(wqk[:, 0], matrix(0, 0), "wqk_loaded")
            load(wqk[:, 1], matrix(0, 1), "wqk_loaded")
            load(wv[:], matrix(0, 2), "wv_loaded")
            sp.wait_ge(S["out_done"], NB * 4)
            load(wo[:], matrix(0, 3), "wo_loaded")
            sp.wait_ge(S["gtr_copied"], NB * 2)
            load(gate_dram.rearrange("e b i n -> e (b i n)"), gatesT, "gate_stored")
            sp.wait_ge(S["gate_stored"], 16)
            load_gates(0, 0)

            def expert(e, last):
                for b in range(NB):
                    s = step(e, b)
                    if isinstance(e, int) and e == 0 and b == 0:
                        load_gates(e, 1)
                    else:
                        regroup(s - 1)
                        if b < NB - 1:
                            load_gates(e, b + 1)
                        elif not last:
                            load_gates(e + 1, 0)
                    if b == 0 and not (isinstance(e, int) and e == 0):
                        sp.wait_ge(S["out_done"], s * 4)
                        load(wo[:], matrix(e, 3), "wo_loaded")
                    if b == NB - 2 and not last:
                        sp.wait_ge(S["q_done"], (s + 1) * HG + HG)
                        sp.wait_ge(S["k_done"], (s + 1) * HG + HG)
                        load(wqk[:, 0], matrix(e + 1, 0), "wqk_loaded")
                        load(wqk[:, 1], matrix(e + 1, 1), "wqk_loaded")
                    if b == NB - 1 and not last:
                        sp.wait_ge(S["v_done"], s * PAIRS + PAIRS)
                        load(wv[:], matrix(e + 1, 2), "wv_loaded")

            expert(0, False)
            with sp.Fori(1, NE - 1) as e:
                expert(e, False)
            expert(NE - 1, True)
            regroup(step(NE - 1, NB - 1))
            for b in range(NB):
                sp.wait_ge(S["out_added"], step(NE - 1, b) * 4 + 4)
                load(out[b], h[:, b], "out_stored")
            sp.wait_ge(S["out_stored"], NB * 16)

        @block.tensor
        def _(pe):
            mm = nc.tensor.matmul
            ident = const("ident")

            def product(o, pairs):
                for k, (lhsT, rhs) in enumerate(pairs):
                    last = mm(o, lhsT, rhs, start=(k == 0), stop=(k == len(pairs) - 1))
                return last

            def patches(b):
                pe.wait_ge(S["x_loaded"], b * 16 + 16)
                for j in range(4):
                    i, m = j // 2, j % 2
                    if b:
                        pe.wait_ge(S["h_ready"], (b - 1) * 4 + j + 1)
                    product(bank[j][:, 0:HALF], [(tokw[:, c, m * P:(m + 1) * P], xpix[b % 2][:, c, half(i)]) for c in range(FC)])\
                        .then_inc(S["patch_done"], 1)

            def means(n, b):
                for i in range(2):
                    u = n * 8 + b * 2 + i
                    if n == 0:
                        pe.wait_ge(S["h_ready"], b * 4 + i * 2 + 2)
                    else:
                        pe.wait_ge(S["out_added"], b * 4 + 4)
                    if u >= 2:
                        pe.wait_ge(S["centered"], (u - 1) * 2)
                    product(bank[4 + i][:, 0:HALF], [(const("mean_d"), h[:, b, c, half(i)]) for c in range(KC)])\
                        .then_inc(S["mean_done"], 1)

            def variances(n, b):
                for i in range(2):
                    u = n * 8 + b * 2 + i
                    pe.wait_ge(S["squared"], u + 1)
                    if u >= 2:
                        pe.wait_ge(S["std_ready"], u - 1)
                    product(bank[6 + i][:, 0:HALF], [(const("mean_d"), sq[:, c, half(i)]) for c in range(KC)])\
                        .then_inc(S["var_done"], 1)

            def output_bias():
                pe.wait_ge(S["oW_loaded"], 16)
                for m in range(KC):
                    for e in range(NE):
                        last = product(bank[7][:, 400 + m * NE + e:401 + m * NE + e],
                                       [(oW_all[:, e, c, m * P:(m + 1) * P], vbT[:, c, e:e + 1]) for c in range(KC)])
                last.then_inc(S["obcol_mm"], 1)
                pe.wait_ge(S["obcol_copied"], 1)
                for m in range(KC):
                    last = nc.tensor.transpose(bank[7][0:NE, m * P:(m + 1) * P], obias_col[:, m, :], ident)
                last.then_inc(S["obias_tr"], 1)
                pe.wait_ge(S["obias_made"], 1)

            pe.wait_ge(S["small_loaded"], NSMALL * 16)
            patches(0)
            output_bias()
            for k in range(1, NB + 2):
                if k < NB:
                    patches(k)
                if k <= NB:
                    means(0, k - 1)
                if k >= 2:
                    variances(0, k - 2)

            def project_qk(s, b, g, rope, waits):
                if g == 0:
                    if rope:
                        pe.wait_ge(S["normed"], b * 4 + 4)
                        if b == 0:
                            pe.wait_ge(S["rope_w_loaded"], 6 * 16)
                    elif b == 0:
                        pe.wait_ge(S["wqk_loaded"], (s - S2) * (32 // NB) + 32)
                for t, (done, wait) in enumerate(zip(("q_done", "k_done"), waits)):
                    if wait:
                        pe.wait_ge(S[wait[0]], wait[1])
                    for w, o in ((wqk[:, t], proj[t]), (wrot[:, :, t * D:(t + 1) * D], maxb[t]))[:2 if rope else 1]:
                        for i in range(2):
                            last = product(o[i * 64:(i + 1) * 64, 0:HALF],
                                           [(w[:, c, g * 64:(g + 1) * 64], xn[:, b, c, half(i)]) for c in range(KC)])
                    last.then_inc(S[done], 1)

            def project_v(s, b, p, rope, wait):
                if wait:
                    pe.wait_ge(S[wait[0]], wait[1])
                if p == 0 and b == 0 and not rope:
                    pe.wait_ge(S["wv_loaded"], (s - S2) * (16 // NB) + 16)
                for i in range(2):
                    at = i * HALF + p * T
                    last = product(proj[p % 2][i * SLOT:i * SLOT + T, 0:D], [(xn[:, b, c, at:at + T], wv[:, c, :]) for c in range(KC)])
                last.then_inc(S["v_done"], 1)

            def project_out(s, b, j, wait, first):
                if j == 0:
                    pe.wait_ge(S["ot_loaded"], s * 64 + 64)
                    if b == 0 and not first:
                        pe.wait_ge(S["wo_loaded"], (s - S2) * (16 // NB) + 16)
                if wait:
                    pe.wait_ge(S[wait[0]], wait[1])
                m, i = j // 2, j % 2
                product(proj[j % 2][:, 0:HALF], [(wo[:, c, m * P:(m + 1) * P], OT[:, c, half(i)]) for c in range(KC)])\
                    .then_inc(S["out_done"], 1)

            def maxima(s, b, p):
                if p == 0:
                    pe.wait_ge(S["q_free"], s * HG + HG)
                    pe.wait_ge(S["k_prep"], s * HG + HG)
                    if isinstance(s, int) and s == 0:
                        pe.wait_ge(S["zeroed"], 6)
                for u in range(2):
                    if not (isinstance(s, int) and s == 0 and p == 0):
                        pe.wait_ge(S["max_ready"], s * 16 + 2 * p - 1 + u)
                    for k in range(2):
                        g = 2 * u + k
                        last = mm(maxb[u][:, k * HT:(k + 1) * HT], QP[:, b % 2, g, p, :], KH[:, b % 2, g, p, :], start=True, stop=True)
                    last.then_inc(S["max_mm"], 1)

            def scores(s, b, p):
                pe.wait_ge(S["maxdiag_ready"], s * PAIRS + p + 1)
                for u in range(2):
                    if not (isinstance(s, int) and s == 0 and p == 0):
                        pe.wait_ge(S["exp_done"], s * 16 + 2 * p - 1 + u)
                    mm(scb[u][:, 0:2 * HT], same_image[:], maxdiag[:, p % 4, u * 8:(u + 1) * 8, :].rearrange("p h t -> p (h t)"),
                       start=True, stop=False)
                    for k in range(2):
                        g = 2 * u + k
                        last = mm(scb[u][:, k * HT:(k + 1) * HT], KP[:, b % 2, g, p, :], QH[:, b % 2, g, p, :], start=False, stop=k == 1)
                    last.then_inc(S["score_done"], 1)

            def values(s, p):
                pe.wait_ge(S["exp_done"], s * 16 + 2 * p + 2)
                pe.wait_ge(S["v_free"], s * PAIRS + p + 1)
                if not (isinstance(s, int) and s == 0 and p < 2):
                    pe.wait_ge(S["o_ready"], s * PAIRS + p - 1)
                o = valb[p % 2]
                for hh in range(HH):
                    for g in range(HG):
                        n = g * HH + hh
                        mm(o[g * 32:(g + 1) * 32, hh * T:(hh + 1) * T],
                           VP[:, p, n].rearrange("k d i -> k (d i)"), probs[:, p % 2, n, :], start=True, stop=True)
                for g in range(HG):
                    last = mm(o[g * 32:(g + 1) * 32, HT:2 * HT], const("ones_pair"),
                              probs[:, p % 2, g * HH:(g + 1) * HH, :].rearrange("p h t -> p (h t)"), start=True, stop=True)
                last.then_inc(S["pv_done"], 1)

            def attend(s, b, follows, nxt, rope, out_prev, outs_before=False):
                n, nb = s + 1, nxt

                def outputs(j, *waits):
                    if nxt is None:
                        waits = (("v_free", s * PAIRS + 7), ("v_free", s * PAIRS + 8)) if j == 0 else \
                            (("out_added", (s - 1) * 4 + 1), ("out_added", (s - 1) * 4 + 2))
                    for k in range(2):
                        project_out(s - 1, (b - 1) % NB, j + k, waits[k], rope)

                if not follows:
                    maxima(s, b, 0)
                    maxima(s, b, 1)
                for p in range(PAIRS):
                    if p + 2 < PAIRS:
                        maxima(s, b, p + 2)
                    elif nxt is not None and not rope:
                        maxima(n, nb, p + 2 - PAIRS)
                    scores(s, b, p)
                    if nxt is not None and p == 5:
                        project_v(n, nb, 2, rope, ("v_free", n * PAIRS + 1))
                        project_v(n, nb, 3, rope, ("v_free", n * PAIRS + 2))
                    if out_prev and p == 7:
                        outputs(2, ("v_free", n * PAIRS + 5), ("v_free", n * PAIRS + 6))
                    if p:
                        values(s, p - 1)
                    elif follows:
                        values(s - 1, PAIRS - 1)
                    if p == 0:
                        project_v(s, b, 7, rope, ("out_added", (s - 2) * 4 + 4) if outs_before else ("v_free", s * PAIRS + 6))
                    if nxt is not None and p < HG:
                        project_qk(n, nb, p, rope, (("v_free", s * PAIRS + 7), ("v_free", s * PAIRS + 8)) if p == 0 else
                                   (("q_free", n * HG + p), ("k_free", n * HG + p)))
                    if nxt is not None and p == 4:
                        project_v(n, nb, 0, rope, ("q_free", n * HG + HG))
                        project_v(n, nb, 1, rope, ("k_free", n * HG + HG))
                    if out_prev and p == 5:
                        outputs(0, ("v_free", n * PAIRS + 3), ("v_free", n * PAIRS + 4))
                    if nxt is not None and p == 6:
                        for q in (4, 5):
                            project_v(n, nb, q, rope, ("out_added", (s - 1) * 4 + q - 3) if out_prev else ("v_free", n * PAIRS + q - 1))
                    if nxt is not None and p == 7:
                        project_v(n, nb, 6, rope, ("out_added", (s - 1) * 4 + 3) if out_prev else ("v_free", n * PAIRS + 5))

            def project_all(s, b, rope, waits):
                for g in range(HG):
                    project_qk(s, b, g, rope, waits if g == 0 else (("q_free", s * HG + g), ("k_free", s * HG + g)))
                for p in range(7):
                    project_v(s, b, p, rope, (("q_free", "k_free")[p], s * HG + HG) if p < 2 else ("v_free", s * PAIRS + p - 1))

            for b in range(NB):
                waits = (("out_added", (b - 2) * 4 + 3), ("out_added", (b - 2) * 4 + 4)) if b >= 2 else \
                    (("v_free", 7), ("v_free", 8)) if b else (None, None)
                if b:
                    pe.wait_ge(S["max_ready"], b * 16)
                project_all(b, b, True, waits)
                attend(b, b, False, None, True, b > 0)
                values(b, PAIRS - 1)
            s = NB - 1
            for j in range(4):
                project_out(s, s, j, ("out_added", (s - 1) * 4 + 3 + j) if j < 2 else ("out_added", s * 4 + j - 1), True)

            pe.wait_ge(S["o_ready"], NB * PAIRS)
            for k in range(NB + 1):
                if k < NB:
                    means(1, k)
                if k:
                    variances(1, k - 1)
            for u in range(2 * NB):
                b, i = u // 2, u % 2
                pe.wait_ge(S["normed"], 16 + 4 * b + 4)
                if u >= 2:
                    pe.wait_ge(S["r_ready"], u - 1)
                product(bank[i][:, 0:HALF], [(rw1[:, c, :], xn[:, b, c, half(i)]) for c in range(KC)]).then_inc(S["r_done"], 1)
            for k in range(2 * NB + 2):
                if k < 2 * NB:
                    pe.wait_ge(S["r_ready"], k + 1)
                    if k >= 2:
                        pe.wait_ge(S["rcentered"], k - 1)
                    mm(bank[2 + k % 2][:, 0:HALF], const("mean_r"), r[:, half(k)], start=True, stop=True).then_inc(S["rmean_done"], 1)
                if k >= 2:
                    u = k - 2
                    pe.wait_ge(S["rsquared"], u + 1)
                    if u >= 2:
                        pe.wait_ge(S["rstd_done"], u - 1)
                    mm(bank[4 + u % 2][:, 0:HALF], const("mean_r"), rsq[:, half(u)], start=True, stop=True).then_inc(S["rvar_done"], 1)
            for t in range(NT):
                pe.wait_ge(S["r_relu"], t // 3 + 1)
                o = bank[0][0:RT, t * NE:(t + 1) * NE]
                mm(o, r[:, t * RT:(t + 1) * RT], rw2[:], start=True, stop=False)
                last = mm(o, const("ones", 1)[:, 0:RT], rb2_row[:], start=False, stop=True)
            last.then_inc(S["logit_done"], 1)
            pe.wait_ge(S["gates_ready"], 1)
            for u in range(2 * NB):
                if u >= 4:
                    pe.wait_ge(S["gtr_copied"], u - 3)
                for t in range(3):
                    last = nc.tensor.transpose(bank[u % 4][0:NE, t * RT:(t + 1) * RT], gates[:, u * 3 + t, :], ident[0:RT, 0:RT])
                last.then_inc(S["gtr_done"], 1)
            for n in range(4 * NB):
                b, m, i = n // 4, n // 2 % 2, n % 2
                pe.wait_ge(S["gtr_copied"], 2 * b + i + 1)
                if n >= 4:
                    pe.wait_ge(S["gobias_added"], n - 3)
                mm(bank[4 + n % 4][:, 0:HALF], obias[:, m * P:(m + 1) * P], gatesT[:, half(2 * b + i)],
                   start=True, stop=True).then_inc(S["gobias_done"], 1)
            pe.wait_ge(S["gobias_added"], 4 * NB)
            pe.wait_ge(S["gate_stored"], 16)

            project_all(S2, 0, False, (("gtr_copied", 2 * NB), ("gtr_copied", 2 * NB)))

            def expert(e, first, last_one):
                for b in range(NB):
                    s = step(e, b)
                    nxt = (b + 1) % NB if not (last_one and b == NB - 1) else None
                    attend(s, b, not (first and b == 0), nxt, False, not (first and b == 0), not (first and b < 2))

            expert(0, True, False)
            with pe.Fori(1, NE - 1) as e:
                expert(e, False, False)
            expert(NE - 1, False, True)
            s = step(NE - 1, NB - 1)
            values(s, PAIRS - 1)
            for j in range(4):
                project_out(s, NB - 1, j, ("out_added", (s - 1) * 4 + 3 + j) if j < 2 else ("out_added", s * 4 + j - 1), False)

        @block.scalar
        def _(act):
            act_f = nc.scalar.activation
            hmask = const("hmask")

            act.wait_ge(S["small_loaded"], NSMALL * 16)

            def squares(n, b):
                for i in range(2):
                    u = n * 8 + b * 2 + i
                    act.wait_ge(S["centered"], (u + 1) * 2)
                    if u >= 2:
                        act.wait_ge(S["var_done"], u - 1)
                    act_f(sq[:, :, half(i)], xn[:, b, :, half(i)], ACT.Square).then_inc(S["squared"], 1)

            def roots(n, b):
                for i in range(2):
                    u = n * 8 + b * 2 + i
                    act.wait_ge(S["var_done"], u + 1)
                    if u >= 2:
                        act.wait_ge(S["rstd_ready"], u - 1)
                    act_f(std[:, i], bank[6 + i][:, 0:HALF], ACT.Sqrt, bias=const("eps"), scale=1.0).then_inc(S["std_ready"], 1)

            for k in range(NB + 2):
                if k < NB:
                    for j in range(4):
                        i, m = j // 2, j % 2
                        act.wait_ge(S["patch_done"], k * 4 + j + 1)
                        act_f(h[:, k, m, half(i)], bank[j][:, 0:HALF], ACT.Identity, bias=tokb[:, m:m + 1], scale=1.0)\
                            .then_inc(S["h_ready"], 1)
                if 1 <= k <= NB:
                    squares(0, k - 1)
                if k >= 2:
                    roots(0, k - 2)

            def prepare_q(s, b, g, rope):
                src = by_token(rope_q if rope else proj[0][:, 0:HALF])
                bias = bias_none if rope else bias_cur
                if rope:
                    act.wait_ge(S["rope_q_ready"], b * HG + g + 1)
                else:
                    act.wait_ge(S["q_done"], s * HG + g + 1)
                for hh in range(HH):
                    act_f(QH[:, b % 2, g, :, hh * T:(hh + 1) * T], src, ACT.Identity,
                          bias=bias[:, g * HH + hh:g * HH + hh + 1], scale=hmask[:, hh:hh + 1])
                for i in range(2):
                    lo, hi = i * 64, (i + 1) * 64
                    last = act_f(QP[lo:hi, b % 2, g, :, i * SLOT:i * SLOT + T], src[lo:hi], ACT.Identity,
                                 bias=bias[lo:hi, 16 + g:17 + g], scale=1.0)
                last.then_inc(S["q_free"], 1)

            def copy_v(s, p):
                act.wait_ge(S["v_done"], s * PAIRS + p + 1)
                for i in range(2):
                    rows_ = slice(i * SLOT, i * SLOT + T)
                    last = act_f(VP[rows_, p, :, :, i], proj[p % 2][rows_, 0:D].rearrange("k (n d) -> k n d", d=HD), ACT.Copy)
                last.then_inc(S["v_free"], 1)

            def exps(s, p):
                for u in range(2):
                    act.wait_ge(S["score_done"], s * 16 + 2 * p + u + 1)
                    if u == 0 and not (isinstance(s, int) and s == 0 and p < 2):
                        act.wait_ge(S["pv_done"], s * PAIRS + p - 1)
                    act_f(probs[:, p % 2, u * 8:(u + 1) * 8, :], scb[u][:, 0:2 * HT].rearrange("p (h t) -> p h t", t=T),
                          ACT.Exp, scale=HD ** -0.5).then_inc(S["exp_done"], 1)

            def attend(s, b, nxt):
                for p in range(PAIRS):
                    exps(s, p)
                    if p == 0:
                        copy_v(s, 7)
                    if nxt is not None and p < HG:
                        if p == 0 and nxt == 0:
                            act.wait_ge(S["bias_ready"], (s + 1 - S2) // NB + 1 if isinstance(s, int) else bias_count[0])
                        prepare_q(s + 1, nxt, p, False)
                    if nxt is not None and p >= HG:
                        for q in range(2 * (p - HG), min(2 * (p - HG) + 2, PAIRS - 1)):
                            copy_v(s + 1, q)

            bias_count = [None]
            act.wait_ge(S["zeroed"], 6)
            for b in range(NB):
                for g in range(HG):
                    prepare_q(b, b, g, True)
                for p in range(7):
                    copy_v(b, p)
                attend(b, b, None)

            for k in range(NB + 1):
                if k < NB:
                    squares(1, k)
                if k:
                    roots(1, k - 1)
            for u in range(2 * NB):
                act.wait_ge(S["r_done"], u + 1)
                act_f(r[:, half(u)], bank[u % 2][:, 0:HALF], ACT.Identity, bias=rvec[:, 0:1], scale=1.0).then_inc(S["r_ready"], 1)
            for k in range(2 * NB + 1):
                if k < 2 * NB:
                    act.wait_ge(S["rcentered"], k + 1)
                    act_f(rsq[:, half(k)], r[:, half(k)], ACT.Square).then_inc(S["rsquared"], 1)
                if k:
                    u = k - 1
                    act.wait_ge(S["rvar_done"], u + 1)
                    if u >= 2:
                        act.wait_ge(S["rrstd"], u - 1)
                    act_f(std[:, u % 2], bank[4 + u % 2][:, 0:HALF], ACT.Sqrt, bias=const("eps"), scale=1.0).then_inc(S["rstd_done"], 1)
            for u in range(2 * NB):
                act.wait_ge(S["r_normed"], u + 1)
                act_f(r[:, half(u)], r[:, half(u)], ACT.Relu, bias=rvec[:, 2:3], scale=rvec[:, 1:2]).then_inc(S["r_relu"], 1)
            act.wait_ge(S["gstep"], 2)
            act_f(lg[:, 1], lg[:, 0], ACT.Exp).then_inc(S["gexp"], 1)

            act.wait_ge(S["bias_ready"], 1)
            for g in range(HG):
                prepare_q(S2, 0, g, False)
            for p in range(7):
                copy_v(S2, p)

            def expert(e, last_one):
                bias_count[0] = e + 2
                for b in range(NB):
                    attend(step(e, b), b, (b + 1) % NB if not (last_one and b == NB - 1) else None)

            expert(0, False)
            with act.Fori(1, NE - 1) as e:
                expert(e, False)
            expert(NE - 1, True)

        @block.vector
        def _(dve):
            v = nc.vector
            hmask = const("hmask")

            v.memset(bias_none[:], 0.0).then_inc(S["zeroed"], 1)
            dve.wait_ge(S["small_loaded"], NSMALL * 16)
            v.tensor_copy(same_image[:], const("same_image")).then_inc(S["cast_done"], 1)
            for g in range(HG):
                for hh in range(HH):
                    last = v.tensor_scalar(bias_all[:, :, g * HH + hh], bias_all[:, :, 16 + g], hmask[:, hh:hh + 1], None, ALU.mult)
            last.then_inc(S["bias_masked"], 1)
            dve.wait_ge(S["obcol_mm"], 1)
            v.tensor_copy(obias_col[:].rearrange("p m e -> p (m e)"), bank[7][:, 400:400 + KC * NE]).then_inc(S["obcol_copied"], 1)
            dve.wait_ge(S["obias_tr"], 1)
            v.tensor_tensor(obias[:], bank[7][0:NE, 0:D], ob_nat[:], ALU.add).then_inc(S["obias_made"], 1)

            def center(n, b):
                for i in range(2):
                    dve.wait_ge(S["mean_done"], n * 8 + b * 2 + i + 1)
                    for c in range(KC):
                        v.tensor_tensor(xn[:, b, c, half(i)], h[:, b, c, half(i)], bank[4 + i][:, 0:HALF],
                                        ALU.subtract).then_inc(S["centered"], 1)

            def scale(n, b):
                for i in range(2):
                    u = n * 8 + b * 2 + i
                    dve.wait_ge(S["std_ready"], u + 1)
                    if u >= 2:
                        dve.wait_ge(S["normed"], (u - 1) * 2)
                    v.reciprocal(rstd[:, i], std[:, i]).then_inc(S["rstd_ready"], 1)
                    dve.wait_ge(S["rstd_ready"], u + 1)
                    for c in range(KC):
                        xs = xn[:, b, c, half(i)]
                        v.tensor_tensor(xs, xs, rstd[:, i], ALU.mult).then_inc(S["normed"], 1)

            for k in range(1, NB + 2):
                if k <= NB:
                    center(0, k - 1)
                if k >= 2:
                    scale(0, k - 2)

            def rope_sum(s, b, g):
                cos = const("cos").unsqueeze(1).to_broadcast([P, PAIRS, T])
                sin = const("sin").unsqueeze(1).to_broadcast([P, PAIRS, T])
                for t, (done, dst, ready) in enumerate((("q_done", rope_q, "rope_q_ready"), ("k_done", rope_k, "rope_k_ready"))):
                    dve.wait_ge(S[done], s * HG + g + 1)
                    n = s * HG + g
                    if n:
                        dve.wait_ge(S[ready], n)
                    v.tensor_tensor(by_token(rope_a[:, t]), by_token(proj[t][:, 0:HALF]), cos, ALU.mult).then_inc(S["rope_part"], 1)
                    v.tensor_tensor(by_token(rope_b[:, t]), by_token(maxb[t][:, 0:HALF]), sin, ALU.mult).then_inc(S["rope_part"], 1)
                    dve.wait_ge(S["rope_part"], (n * 2 + t) * 2 + 2)
                    if t == 0 and n:
                        dve.wait_ge(S["q_free"], n)
                    if t == 1 and n:
                        dve.wait_ge(S["k_free"], n)
                    v.tensor_tensor(dst, rope_a[:, t], rope_b[:, t], ALU.add).then_inc(S[ready], 1)
                dve.wait_ge(S["rope_k_ready"], n + 1)

            def prepare_k(s, b, g, rope):
                src = by_token(rope_k if rope else proj[1][:, 0:HALF])
                bias = bias_none if rope else bias_cur
                if rope:
                    rope_sum(s, b, g)
                else:
                    dve.wait_ge(S["k_done"], s * HG + g + 1)
                for i in range(2):
                    lo, hi = i * 64, (i + 1) * 64
                    v.tensor_scalar(KP[lo:hi, b % 2, g, :, i * SLOT:i * SLOT + T], src[lo:hi], bias[lo:hi, 20 + g:21 + g], None, ALU.add)
                if not (isinstance(s, int) and s == 0 and g == 0):
                    dve.wait_ge(S["k_prep"], s * HG + g)
                v.tensor_scalar(by_token(Kb[:]), src, bias[:, 20 + g:21 + g], None, ALU.add).then_inc(S["k_free"], 1)
                dve.wait_ge(S["k_free"], s * HG + g + 1)
                for hh in range(HH):
                    last = v.tensor_scalar(KH[:, b % 2, g, :, hh * T:(hh + 1) * T], by_token(Kb[:]), hmask[:, hh:hh + 1], None, ALU.mult)
                last.then_inc(S["k_prep"], 1)

            def add_out(s, b, j, bias):
                m, i = j // 2, j % 2
                dve.wait_ge(S["out_done"], s * 4 + j + 1)
                hs = h[:, b, m, half(i)]
                if bias is None:
                    last = v.tensor_tensor(hs, proj[j % 2][:, 0:HALF], hs, ALU.add)
                else:
                    last = v.scalar_tensor_tensor(out=hs, in0=proj[j % 2][:, 0:HALF], scalar=bias[:, m:m + 1], in1=hs,
                                                  op0=ALU.add, op1=ALU.add)
                last.then_inc(S["out_added"], 1)

            def reduce_max(s, p):
                if not (isinstance(s, int) and s == 0 and p < 4):
                    dve.wait_ge(S["maxdiag_ready"], s * PAIRS + p - 3)
                for u in range(2):
                    dve.wait_ge(S["max_mm"], s * 16 + 2 * p + u + 1)
                    v.tensor_reduce(rowmax[:, p % 4, u * 8:(u + 1) * 8], maxb[u][:, 0:2 * HT].rearrange("p (h t) -> p h t", t=T), AX,
                                    ALU.max).then_inc(S["max_ready"], 1)

            def normalize(s, b, p, gated):
                n = s * PAIRS + p
                dve.wait_ge(S["pv_done"], n + 1)
                if not (isinstance(s, int) and s == 0 and p < 2):
                    dve.wait_ge(S["o_ready"], n - 1)
                o = valb[p % 2]
                v.reciprocal(rsum[:, p % 2], o[:, HT:2 * HT].rearrange("p (h t) -> p h t", t=T)).then_inc(S["rsum_ready"], 1)
                if p == 0 and not (isinstance(s, int) and s == 0):
                    dve.wait_ge(S["ot_loaded"], s * 64)
                dve.wait_ge(S["rsum_ready"], n + 1)
                factor = rsum
                if gated:
                    if p == 0:
                        dve.wait_ge(S[f"gate_loaded{b % 2}"], (s - b - S2) * 16 + b // 2 * 32 + 32)
                    v.tensor_tensor(scale_o[:, p % 2], rsum[:, p % 2], gate_rep[:, b % 2, p:p + 1, :].to_broadcast([P, HH, T]),
                                    ALU.mult).then_inc(S["scale_ready"], 1)
                    dve.wait_ge(S["scale_ready"], n - S2 * PAIRS + 1)
                    factor = scale_o
                v.tensor_tensor(ON[:, :, p, :], o[:, 0:HT].rearrange("p (h t) -> p h t", t=T), factor[:, p % 2],
                                ALU.mult).then_inc(S["o_ready"], 1)

            def attend(s, b, follows, nxt, rope, out_prev):
                def outputs(j):
                    for k in range(2):
                        add_out(s - 1, (b - 1) % NB, j + k, bout if rope else None)

                if not follows:
                    reduce_max(s, 0)
                    reduce_max(s, 1)
                for p in range(PAIRS):
                    if p + 2 < PAIRS:
                        reduce_max(s, p + 2)
                    elif nxt is not None:
                        reduce_max(s + 1, p + 2 - PAIRS)
                    if out_prev and p == 7:
                        outputs(2)
                    if p:
                        normalize(s, b, p - 1, not rope)
                    elif follows:
                        normalize(s - 1, (b - 1) % NB, PAIRS - 1, not rope)
                    if nxt is not None and p < HG:
                        if p == 0 and nxt == 0:
                            dve.wait_ge(S["bias_ready"], bias_count[0])
                        prepare_k(s + 1, nxt, p, False)
                    if out_prev and p == 5:
                        outputs(0)

            bias_count = [None]
            dve.wait_ge(S["zeroed"], 6)
            for b in range(NB):
                for g in range(HG):
                    prepare_k(b, b, g, True)
                attend(b, b, False, None, True, b > 0)
                normalize(b, b, PAIRS - 1, False)
            for j in range(4):
                add_out(NB - 1, NB - 1, j, bout)

            for k in range(NB + 1):
                if k < NB:
                    center(1, k)
                if k:
                    scale(1, k - 1)
            for k in range(2 * NB + 1):
                if k < 2 * NB:
                    dve.wait_ge(S["rmean_done"], k + 1)
                    v.tensor_tensor(r[:, half(k)], r[:, half(k)], bank[2 + k % 2][:, 0:HALF], ALU.subtract).then_inc(S["rcentered"], 1)
                if k:
                    u = k - 1
                    dve.wait_ge(S["rstd_done"], u + 1)
                    if u >= 2:
                        dve.wait_ge(S["r_normed"], u - 1)
                    v.reciprocal(rstd[:, u % 2], std[:, u % 2]).then_inc(S["rrstd"], 1)
                    dve.wait_ge(S["rrstd"], u + 1)
                    v.tensor_tensor(r[:, half(u)], r[:, half(u)], rstd[:, u % 2], ALU.mult).then_inc(S["r_normed"], 1)

            done = [0]

            def then(ins):
                done[0] += 1
                ins.then_inc(S["gstep"], 1)
                dve.wait_ge(S["gstep"], done[0])

            wide = lambda a: a.unsqueeze(2).to_broadcast([RT, NT, NE])
            dve.wait_ge(S["logit_done"], 1)
            logits = bank[0][0:RT, 0:NT * NE].rearrange("p (t e) -> p t e", e=NE)
            then(v.tensor_reduce(rs[:, 0], logits, AX, ALU.max))
            then(v.tensor_tensor(lg[:, 0], logits, wide(rs[:, 0]), ALU.subtract))
            dve.wait_ge(S["gexp"], 1)
            then(v.tensor_reduce(rs[:, 1], lg[:, 1], AX, ALU.add))
            then(v.reciprocal(rs[:, 2], rs[:, 1]))
            then(v.tensor_tensor(lg[:, 2], lg[:, 1], wide(rs[:, 2]), ALU.mult))
            for t in range(NT):
                last = v.max(top[:, t, :], lg[:, 2, t, :])
            then(last)
            for t in range(NT):
                last = v.max_index(topi[:, t, :], top[:, t, :], lg[:, 2, t, :])
            then(last)
            then(v.tensor_copy(topf[:], topi[:]))
            then(v.tensor_tensor(rs[:, 3], top[:, :, 0], top[:, :, 1], ALU.add))
            then(v.reciprocal(rs[:, 0], rs[:, 3]))
            iota = const("iota", RT).rearrange("p (t e) -> p t e", e=NE)
            for k in range(2):
                then(v.tensor_tensor(gsel[:, k], iota, wide(topf[:, :, k]), ALU.is_equal))
                then(v.tensor_tensor(gsel[:, k], gsel[:, k], wide(top[:, :, k]), ALU.mult))
            then(v.tensor_tensor(lg[:, 3], gsel[:, 0], gsel[:, 1], ALU.add))
            v.tensor_tensor(gates[:], lg[:, 3], wide(rs[:, 0]), ALU.mult).then_inc(S["gates_ready"], 1)
            for u in range(2 * NB):
                dve.wait_ge(S["gtr_done"], u + 1)
                v.tensor_copy(gatesT[:, half(u)], bank[u % 4][0:NE, 0:HALF]).then_inc(S["gtr_copied"], 1)
            for n in range(4 * NB):
                b, m, i = n // 4, n // 2 % 2, n % 2
                dve.wait_ge(S["gobias_done"], n + 1)
                hs = h[:, b, m, half(i)]
                v.tensor_tensor(hs, bank[4 + n % 4][:, 0:HALF], hs, ALU.add).then_inc(S["gobias_added"], 1)

            dve.wait_ge(S["bias_ready"], 1)
            for g in range(HG):
                prepare_k(S2, 0, g, False)

            def expert(e, first, last_one):
                bias_count[0] = e + 2
                for b in range(NB):
                    nxt = (b + 1) % NB if not (last_one and b == NB - 1) else None
                    attend(step(e, b), b, not (first and b == 0), nxt, False, not (first and b == 0))

            expert(0, True, False)
            with dve.Fori(1, NE - 1) as e:
                expert(e, False, False)
            expert(NE - 1, False, True)
            s = step(NE - 1, NB - 1)
            normalize(s, NB - 1, PAIRS - 1, True)
            for j in range(4):
                add_out(s, NB - 1, j, None)

        @block.gpsimd
        def _(pool):
            g_ = nc.gpsimd
            g_.memset(QP[:, 0].bitcast(F32), 0.0).then_inc(S["zeroed"], 1)
            g_.memset(QP[:, 1].bitcast(F32), 0.0).then_inc(S["zeroed"], 1)
            g_.memset(VP[:], 0.0).then_inc(S["zeroed"], 1)
            pool.wait_ge(S["small_loaded"], NSMALL * 16)
            pool.wait_ge(S["obcol_mm"], 1)
            g_.memset(KP[:, 0], 0.0).then_inc(S["zeroed"], 1)
            pool.wait_ge(S["patch_done"], 4 * NB)
            g_.memset(KP[:, 1], 0.0).then_inc(S["zeroed"], 1)

            def diagonal(s, p):
                pool.wait_ge(S["max_ready"], s * 16 + 2 * p + 2)
                if not (isinstance(s, int) and s == 0 and p < 4):
                    pool.wait_ge(S["score_done"], s * 16 + 2 * (p - 3))
                g_.tensor_tensor(maxdiag[:, p % 4], rowmax[:, p % 4].unsqueeze(2).to_broadcast([P, HEADS, T]),
                                 const("negdiag").unsqueeze(1).to_broadcast([P, HEADS, T]), ALU.mult).then_inc(S["maxdiag_ready"], 1)

            def load_bias(e):
                src = bias_all[:, e] if isinstance(e, int) else bias_all[:, bass.ds(e, 1), :].rearrange("p o n -> p (o n)")
                g_.tensor_copy(bias_cur[:], src).then_inc(S["bias_ready"], 1)

            pool.wait_ge(S["bias_masked"], 1)
            load_bias(0)
            for b in range(NB):
                for p in range(PAIRS):
                    diagonal(b, p)

            def expert(e, last_one):
                for b in range(NB):
                    s = step(e, b)
                    for p in range(PAIRS):
                        diagonal(s, p)
                        if b == NB - 2 and p == 6 and not last_one:
                            pool.wait_ge(S["q_free"], (s + 1) * HG + HG)
                            pool.wait_ge(S["k_free"], (s + 1) * HG + HG)
                            load_bias(e + 1)

            expert(0, False)
            with pool.Fori(1, NE - 1) as e:
                expert(e, False)
            expert(NE - 1, True)


def rows(a, n=P):
    return a.reshape(-1, n, *a.shape[1:]).swapaxes(0, 1)


def kernel(x, L0_tok_W, L0_tok_b, L0_attn_w_qkv, L0_attn_w_out, L0_attn_b_out, L0_ffn_rW1, L0_ffn_rb1, L0_ffn_ln_g,
           L0_ffn_ln_b, L0_ffn_rW2, L0_ffn_rb2, L0_ffn_qW, L0_ffn_qb, L0_ffn_kW, L0_ffn_kb, L0_ffn_vW, L0_ffn_vb,
           L0_ffn_oW, L0_ffn_ob):
    import concourse.bacc as _bacc
    from concourse.bass_utils import run_bass_kernel_spmd as _run

    pixels = np.asarray(x).reshape(NB, BATCH, CHANNELS, GRID, PATCH, GRID, PATCH).transpose(0, 2, 4, 6, 1, 3, 5)
    pixels = pixels.reshape(NB, FC, P, TOK).swapaxes(1, 2)

    def heads_rows(w):
        return np.asarray(w).reshape(HG, 2, 2, HD, -1).transpose(2, 0, 3, 1, 4).reshape(P, KC, -1)

    qkv = np.asarray(L0_attn_w_qkv)
    partner = qkv[:, :2 * D].reshape(D, 2 * HEADS, 2, HD // 2)[:, :, ::-1].reshape(D, 2 * D)
    experts = [np.stack([rows(np.asarray(w)[e].T) for w in (L0_ffn_qW, L0_ffn_kW, L0_ffn_vW)]
                        + [heads_rows(np.asarray(L0_ffn_oW)[e].T)], axis=1) for e in range(NE)]
    qkb = np.stack([np.asarray(b).reshape(NE, HG, SLOT) for b in (L0_ffn_qb, L0_ffn_kb)], axis=1)
    qkb = np.concatenate([qkb.transpose(3, 0, 1, 2).reshape(SLOT, NE, 2 * HG)] * 2)
    arrays = {
        "pixels": pixels, "tok_W": rows(np.asarray(L0_tok_W).T), "tok_b": rows(np.asarray(L0_tok_b)),
        "w_qkv": rows(qkv), "w_partner": rows(partner), "w_out": heads_rows(L0_attn_w_out), "b_out": rows(np.asarray(L0_attn_b_out)),
        "rW1": rows(np.asarray(L0_ffn_rW1).T), "rvec": np.stack([np.asarray(a) for a in (L0_ffn_rb1, L0_ffn_ln_g, L0_ffn_ln_b)], axis=1),
        "rW2": np.asarray(L0_ffn_rW2).T, "rb2": np.asarray(L0_ffn_rb2)[None], "experts": np.stack(experts), "qk_bias": qkb,
        "v_bias": heads_rows(np.asarray(L0_ffn_vb).T), "oW": np.stack([e[:, 3] for e in experts], axis=1), "o_bias": np.asarray(L0_ffn_ob), "table": constants(),
    }
    arrays = {k: np.ascontiguousarray(a) for k, a in arrays.items()}
    nc = _bacc.Bacc("TRN2", target_bir_lowering=False, num_devices=1)
    args = [nc.dram_tensor(f"in_{name}", a.shape, mybir.dt.from_np(a.dtype), kind="ExternalInput").ap()
            for name, a in arrays.items()]
    out = nc.dram_tensor("out_h", (NB, P, KC, TOK), F32, kind="ExternalOutput").ap()
    build(nc, *args, out)
    r = _run(nc, [{f"in_{k}": a for k, a in arrays.items()}], core_ids=[0])
    return r.results[0]["out_h"].transpose(0, 3, 2, 1).reshape(IMAGES, T, D)
```

```python
from contextlib import ExitStack

import numpy as np

import concourse.bass as bass
from concourse import mybir

F32 = mybir.dt.float32
BF16 = mybir.dt.bfloat16
U32 = mybir.dt.uint32
ALU = mybir.AluOpType
ACT = mybir.ActivationFunctionType
AX = mybir.AxisListType.X

IMAGES, CHANNELS, SIDE, PATCH = 64, 3, 96, 16
GRID = SIDE // PATCH
T = GRID * GRID
D = 256
HEADS, HD = 16, 16
NE = 8
RH = 128
P = 128
KC = D // P
BATCH = 16
NB = IMAGES // BATCH
PAIRS = BATCH // 2
HALF = PAIRS * T
TOK = BATCH * T
HG, HH = 4, 4
HT = HH * T
SLOT = 64
PAD = SLOT - T
S2 = NB
FC = CHANNELS * PATCH * PATCH // P
NU = NB * 2
NQ = HALF // 4
RT = 96
NT = NB * TOK // RT
EPS = 1e-5

CONSTS = {}
_at = 0
for _n, _w in (("ident", P), ("rotate", P), ("negdiag", T), ("hmask", HH), ("ones_pair", 32), ("mean_d", P), ("mean_r", P),
               ("same_image", P), ("cos", T), ("sin", T), ("iota", NE), ("eps", 1), ("spread", 4 * P)):
    CONSTS[_n] = (_at, _at + _w)
    _at += _w
CW = _at


def constants():
    t = np.zeros((P, CW), np.float32)
    row = np.arange(P)

    def put(name, a):
        lo, hi = CONSTS[name]
        t[:, lo:hi] = a

    put("ident", np.eye(P))
    put("rotate", row[:, None] == row[None] ^ (HD // 2))
    put("negdiag", -(row[:, None] % SLOT == np.arange(T)[None]).astype(np.float32))
    put("hmask", (row[:, None] % SLOT) // HD == np.arange(HH)[None])
    valid = row % SLOT < T
    put("ones_pair", valid[:, None] & (row[:, None] // SLOT == np.arange(32)[None] % 2))
    put("mean_d", 1.0 / D)
    put("mean_r", 1.0 / RH)
    put("same_image", valid[:, None] & valid[None] & (row[:, None] // SLOT == row[None] // SLOT))
    theta = (1.0 / np.float32(10000.0) ** (np.arange(0, HD, 2, dtype=np.float32) / np.float32(HD))).astype(np.float32)
    angle = np.outer(np.arange(T, dtype=np.float32), theta).astype(np.float32)
    angle = np.concatenate([angle, angle], axis=-1)[:, row % HD].T
    put("cos", np.cos(angle))
    put("sin", np.sin(angle) * np.where(row % HD < HD // 2, -1, 1)[:, None])
    put("iota", np.arange(NE)[None])
    put("spread", np.repeat(row[:, None] == 32 * np.arange(4)[None], P, axis=1))
    put("eps", EPS)
    return t


def build(nc, pixels, tokW, tokB, wqkv1, wout1, bout1, rW1, rvecs, rW2, rb2, wts, qkb, vb, oW, ob, table, out):
    with ExitStack() as ctx:
        def sb(name, shape, dt=F32):
            return ctx.enter_context(nc.sbuf_tensor(name, shape, dt))

        gate_dram = nc.dram_tensor("gate_dram", (NE, NB, 2, HALF), F32).ap()

        ct = sb("ct", [P, CW])

        def const(name, rows=P):
            lo, hi = CONSTS[name]
            return ct[0:rows, lo:hi]

        same_image = sb("same_image", [P, P], BF16)
        tokb = sb("tokb", [P, KC])
        wqk = sb("wqk", [P, 2, KC, D])
        wv = sb("wv", [P, KC, D])
        wo = sb("wo", [P, KC, D])
        bout = sb("bout", [P, KC])
        rw1 = sb("rw1", [P, KC, RH])
        rw2 = sb("rw2", [RH, NE])
        rb2_rep = sb("rb2_rep", [RT, NE])
        rvec = sb("rvec", [RH, 3])
        bias_all = sb("bias_all", [P, NE, 24])
        bias_cur = sb("bias_cur", [P, 24])
        bias_none = sb("bias_none", [P, 24])
        vbT = sb("vbT", [P, KC, NE])
        vb_diag = sb("vb_diag", [P, KC, NE, NE])
        ob_nat = sb("ob_nat", [NE, D])
        obias = sb("obias", [NE, D])

        h = sb("h", [P, NB, KC, TOK])
        xn = sb("xn", [P, NB, KC, TOK])
        sq = sb("sq", [P, KC, TOK])
        std = sb("std", [P, 4, NQ])
        rstd = sb("rstd", [P, 4, NQ])
        QH = sb("QH", [P, 2, HG, PAIRS, HT])
        KP = sb("KP", [P, 2, HG, PAIRS, P])
        KH = sb("KH", [P, 2, HG, PAIRS, HT], BF16)
        QP = sb("QP", [P, 2, HG, PAIRS, P], BF16)
        Kb = sb("Kb", [P, HALF], BF16)
        VP = sb("VP", [P, PAIRS, HEADS, HD, 2])
        VT = sb("VT", [P, KC, PAIRS // 2, 2 * SLOT])
        rowmax = sb("rowmax", [P, 4, HEADS])
        maxdiag = sb("maxdiag", [P, 4, HEADS, T], BF16)
        probs = sb("probs", [P, 2, HEADS, T])
        rsum = sb("rsum", [P, 2, HH, T])
        scale_o = sb("scale_o", [P, 2, HH, T])
        gate_rep = sb("gate_rep", [P, 2, PAIRS, T])
        ON = sb("ON", [P, HH, PAIRS, T])
        OT = sb("OT", [P, KC, TOK])
        raw = scale_o.rearrange("p k h t -> p (k h t)"), sb("raw_k", [P, HALF])[:]
        rope_a, rope_b = sq[:, 0].rearrange("p (t n) -> p t n", t=2), sq[:, 1].rearrange("p (t n) -> p t n", t=2)
        rope_q, rope_k = (gate_rep[:, t].rearrange("p n t -> p (n t)") for t in range(2))

        def room(tile, t, n):
            return tile[:, t].rearrange("p g n t -> p (g n t)")[:, 0:n]

        xpix = [room(QH, t, FC * TOK).rearrange("p (c n) -> p c n", c=FC) for t in range(2)]
        oW_all = room(KP, 0, NE * KC * D).rearrange("p (e c n) -> p e c n", e=NE, c=KC)
        tokw = room(KP, 1, FC * D).rearrange("p (c n) -> p c n", c=FC)
        gatesT = [OT[0:NE].rearrange("p c n -> p (c n)"), sq[0:NE].rearrange("p c n -> p (c n)")]
        r = room(QH, 1, NB * TOK)
        rsq = room(QH, 1, 2 * NB * TOK)[:, NB * TOK:]

        KH_room = KH[0:RT, 1].rearrange("p g n t -> p (g n t)").bitcast(F32)
        _at = [0]

        def small(*shape, dt=F32):
            n = int(np.prod(shape))
            a = KH_room[:, _at[0]:_at[0] + n]
            _at[0] += n
            a = a.bitcast(U32) if dt == U32 else a
            return a if len(shape) == 1 else a.rearrange("p (a b) -> p a b", a=shape[0]) if len(shape) == 2 else \
                a.rearrange("p (a b c) -> p a b c", a=shape[0], b=shape[1])

        lg, rs = small(4, NT, NE), small(4, NT)
        top, topi, topf = small(NT, 8), small(NT, 8, dt=U32), small(NT, 8)
        gsel, gates = small(2, NT, NE), small(NT, NE)

        bank = [ctx.enter_context(nc.psum_tensor(f"bank{i}", [P, 512], F32)) for i in range(8)]
        proj, maxb, scb, valb = bank[0:2], bank[2:4], bank[4:6], bank[6:8]

        S = {n: ctx.enter_context(nc.semaphore(n)) for n in (
            "small_loaded tokw_loaded x_first_loaded oW_loaded rope_w_loaded tiles_ready bias_masked vb_zeroed vb_ready obias_done obias_made "
            "x_loaded patch_done h_ready mean_done centered squared var_done std_ready rstd_ready rep_done normed "
            "bias_ready q_done q_free k_done k_free raw_ready rot_done rope_a_made rope_b_made rope_q_ready rope_k_ready k_prep "
            "vt_done vt_ready v_done v_free gate_loaded0 gate_loaded1 "
            "max_mm max_ready maxdiag_ready score_done exp_done pv_done rsum_ready scale_ready o_ready "
            "ot_loaded out_done out_added wqk_loaded wv_loaded wo_loaded "
            "r_done r_ready rmean_done rcentered rsquared rvar_done rstd_done rrstd rrep_done r_normed r_relu logit_done gstep gexp "
            "gates_ready gtr_done gtr_copied gate_stored gobias_done gobias_added out_stored").split()}

        block = ctx.enter_context(nc.Block())
        NSMALL = 9
        NREADY = 8
        half = lambda i: slice(i * HALF, (i + 1) * HALF)
        by_token = lambda a: a.rearrange("p (n t) -> p n t", t=T)

        def step(e, b):
            return S2 + e * NB + b

        @block.sync
        def _(sp):
            def load(dst, src, s):
                sp.dma_start(dst, src).then_inc(S[s], 16)

            load(tokw, tokW, "tokw_loaded")
            load(xpix[0][:, :, half(0)], pixels[0, :, :, half(0)], "x_first_loaded")
            load(xpix[0][:, :, half(1)], pixels[0, :, :, half(1)], "x_loaded")
            for dst, src in ((ct[:], table), (tokb[:], tokB), (rvec[:], rvecs), (rw1[:], rW1), (rw2[:], rW2),
                             (rb2_rep[:], rb2.partition_broadcast(RT).rearrange("q o n -> q (o n)")),
                             (bias_all[:, :, 16:24], qkb), (vbT[:], vb), (ob_nat[:], ob)):
                load(dst, src, "small_loaded")
            sp.wait_ge(S["x_loaded"], 16)
            load(xpix[1], pixels[1], "x_loaded")
            load(oW_all, oW, "oW_loaded")
            load(wqk[:, 0], wqkv1[:, :, 0:D], "rope_w_loaded")
            load(wqk[:, 1], wqkv1[:, :, D:2 * D], "rope_w_loaded")
            load(wv[:], wqkv1[:, :, 2 * D:3 * D], "rope_w_loaded")
            load(wo[:], wout1, "rope_w_loaded")
            load(bout[:], bout1, "rope_w_loaded")
            for b in range(2, NB):
                sp.wait_ge(S["x_loaded"], b * 16)
                sp.wait_ge(S["patch_done"], (b - 2) * 4 + 4)
                load(xpix[b % 2], pixels[b], "x_loaded")

            def regroup(s):
                sp.wait_ge(S["o_ready"], s * PAIRS + PAIRS)
                for i in range(2):
                    for x_ in range(2):
                        src = ON[i:i + 127:2].rearrange("p (c x) n t -> p x c (n t)", x=2)[:, x_]
                        load(OT[x_ * 64:(x_ + 1) * 64, :, half(i)], src, "ot_loaded")

            def load_gates(e, b):
                for i in range(2):
                    src = gate_dram[bass.ds(e, 1), b, i] if not isinstance(e, int) else gate_dram[e:e + 1, b, i]
                    load(gate_rep[i:i + 127:2, b % 2].rearrange("p n t -> p (n t)"), src.partition_broadcast(64).rearrange("q o n -> q (o n)"),
                         f"gate_loaded{b % 2}")

            def matrix(e, t):
                if isinstance(e, int):
                    return wts[e, :, t]
                return wts[bass.ds(e, 1)].rearrange("o p t c n -> p (o t) c n")[:, t]

            for b in range(NB):
                regroup(b)
            load(wqk[:, 0], matrix(0, 0), "wqk_loaded")
            load(wqk[:, 1], matrix(0, 1), "wqk_loaded")
            load(wv[:], matrix(0, 2), "wv_loaded")
            sp.wait_ge(S["out_done"], NB * 4)
            load(wo[:], matrix(0, 3), "wo_loaded")
            sp.wait_ge(S["gtr_copied"], NB * 2)
            for k in range(2):
                load(gate_dram[:, 2 * k:2 * k + 2].rearrange("e b i n -> e (b i n)"), gatesT[k], "gate_stored")
            sp.wait_ge(S["gate_stored"], 32)
            load_gates(0, 0)

            def store(b):
                for m in range(KC):
                    sp.wait_ge(S["out_added"], step(NE - 1, b) * 4 + 2 * m + 2)
                    load(out[b, :, m], h[:, b, m], "out_stored")

            def expert(e, last):
                for b in range(NB):
                    s = step(e, b)
                    if isinstance(e, int) and e == 0 and b == 0:
                        load_gates(e, 1)
                    else:
                        regroup(s - 1)
                        if b < NB - 1:
                            load_gates(e, b + 1)
                        elif not last:
                            load_gates(e + 1, 0)
                    if b == 0 and not (isinstance(e, int) and e == 0):
                        sp.wait_ge(S["out_done"], s * 4)
                        load(wo[:], matrix(e, 3), "wo_loaded")
                    if b == NB - 2 and not last:
                        sp.wait_ge(S["q_done"], (s + 1) * HG + HG)
                        sp.wait_ge(S["k_done"], (s + 1) * HG + HG)
                        load(wqk[:, 0], matrix(e + 1, 0), "wqk_loaded")
                        load(wqk[:, 1], matrix(e + 1, 1), "wqk_loaded")
                    if last and b >= 2:
                        store(b - 2)
                    if b == NB - 1 and not last:
                        sp.wait_ge(S["v_done"], s * PAIRS + PAIRS)
                        load(wv[:], matrix(e + 1, 2), "wv_loaded")

            expert(0, False)
            with sp.Fori(1, NE - 1) as e:
                expert(e, False)
            expert(NE - 1, True)
            regroup(step(NE - 1, NB - 1))
            store(NB - 2)
            store(NB - 1)
            sp.wait_ge(S["out_stored"], NB * KC * 16)

        @block.tensor
        def _(pe):
            mm = nc.tensor.matmul
            ident = const("ident")

            def product(o, pairs):
                for k, (lhsT, rhs) in enumerate(pairs):
                    last = mm(o, lhsT, rhs, start=(k == 0), stop=(k == len(pairs) - 1))
                return last

            def patches(b, i):
                if b == 0 and i == 0:
                    pe.wait_ge(S["tokw_loaded"], 16)
                    pe.wait_ge(S["x_first_loaded"], 16)
                elif b == 0 or i == 0:
                    pe.wait_ge(S["x_loaded"], b * 16 + 16)
                for m in range(2):
                    j = i * 2 + m
                    if b:
                        pe.wait_ge(S["h_ready"], (b - 1) * 4 + j + 1)
                    product(bank[j][:, 0:HALF], [(tokw[:, c, m * P:(m + 1) * P], xpix[b % 2][:, c, half(i)]) for c in range(FC)])\
                        .then_inc(S["patch_done"], 1)

            def mean(n, u):
                b, i, w = u // 2, u % 2, n * NU + u
                if n == 0:
                    pe.wait_ge(S["h_ready"], u * 2 + 2)
                else:
                    pe.wait_ge(S["out_added"], b * 4 + 4)
                if w >= 2:
                    pe.wait_ge(S["centered"], (w - 1) * 2)
                product(bank[4 + i][:, 0:HALF], [(const("mean_d"), h[:, b, c, half(i)]) for c in range(KC)])\
                    .then_inc(S["mean_done"], 1)

            def variance_of(o, w, terms):
                for k in range(4):
                    last = product(o[k * 32:(k + 1) * 32, 0:NQ], [(w[:, 0:32], t[:, k * NQ:(k + 1) * NQ]) for t in terms])
                return last

            def spread(o, compact):
                for k in range(4):
                    last = mm(o[:, k * NQ:(k + 1) * NQ], const("spread")[:, k * P:(k + 1) * P], compact, start=True, stop=True)
                return last

            def variance(n, u):
                i, w = u % 2, n * NU + u
                pe.wait_ge(S["squared"], w + 1)
                if w >= 2:
                    pe.wait_ge(S["normed"], (w - 1) * 2)
                variance_of(bank[6 + i], const("mean_d"), [sq[:, c, half(i)] for c in range(KC)]).then_inc(S["var_done"], 1)

            def replicate(n, u):
                i, w = u % 2, n * NU + u
                pe.wait_ge(S["rstd_ready"], w + 1)
                spread(bank[6 + i], rstd[:, i]).then_inc(S["rep_done"], 1)

            def output_bias(experts):
                if experts[0] == 0:
                    pe.wait_ge(S["oW_loaded"], 16)
                    pe.wait_ge(S["vb_ready"], 1)
                    pe.wait_ge(S["h_ready"], 4 * NB)
                for e in experts:
                    for c in range(KC):
                        last = mm(bank[3][0:NE, 0:D], vb_diag[:, c, e, :], oW_all[:, e, c, :],
                                  start=(e == 0 and c == 0), stop=(e == NE - 1 and c == KC - 1))
                if experts[-1] == NE - 1:
                    last.then_inc(S["obias_done"], 1)

            for k in range(NU + 3):
                if k == 1:
                    pe.wait_ge(S["small_loaded"], NSMALL * 16)
                if k < NU:
                    patches(k // 2, k % 2)
                if 0 <= k - 1 < NU:
                    mean(0, k - 1)
                if 0 <= k - 2 < NU:
                    variance(0, k - 2)
                if 0 <= k - 3 < NU:
                    replicate(0, k - 3)
                if k in (NU, NU + 1):
                    output_bias(range(NE // 2) if k == NU else range(NE // 2, NE))

            def project_qk(s, b, g, rope, waits):
                if g == 0:
                    if rope:
                        pe.wait_ge(S["normed"], b * 4 + 4)
                        if b == 0:
                            pe.wait_ge(S["rope_w_loaded"], 5 * 16)
                    elif b == 0:
                        pe.wait_ge(S["wqk_loaded"], (s - S2) * (32 // NB) + 32)
                for t, (done, wait) in enumerate(zip(("q_done", "k_done"), waits)):
                    if wait:
                        pe.wait_ge(S[wait[0]], wait[1])
                    for i in range(2):
                        last = product(proj[t][i * 64:(i + 1) * 64, 0:HALF],
                                       [(wqk[:, t, c, g * 64:(g + 1) * 64], xn[:, b, c, half(i)]) for c in range(KC)])
                    last.then_inc(S[done], 1)

            def rotate(b, g):
                for t in range(2):
                    pe.wait_ge(S["raw_ready"], (b * HG + g) * 2 + t + 1)
                    mm(proj[t][:, 0:HALF], const("rotate"), raw[t], start=True, stop=True).then_inc(S["rot_done"], 1)

            def qk_free(s, g, rope):
                n = s * HG + g + 1
                return (("rope_b_made", n * 2 - 1), ("rope_b_made", n * 2)) if rope else (("q_free", n), ("k_free", n))

            def project_v(s, b, a, rope, waits, banks=proj):
                if a == 0 and b == 0 and not rope:
                    pe.wait_ge(S["wv_loaded"], (s - S2) * (16 // NB) + 16)
                for m in range(KC):
                    if waits[m]:
                        pe.wait_ge(S[waits[m][0]], waits[m][1])
                    for i in range(2):
                        at = i * HALF + a * HT
                        last = product(banks[m][:, i * HT:(i + 1) * HT],
                                       [(wv[:, c, m * P:(m + 1) * P], xn[:, b, c, at:at + HT]) for c in range(KC)])
                    last.then_inc(S["vt_done"], 1)

            def turn_v(s, p, wait, banks=proj):
                if p % 4 == 0:
                    pe.wait_ge(S["vt_ready"], s * 4 + (p // 4) * 2 + 2)
                if wait:
                    pe.wait_ge(S[wait[0]], wait[1])
                for m in range(KC):
                    last = nc.tensor.transpose(banks[p % 2][0:SLOT + T, m * P:(m + 1) * P], VT[:, m, p % 4, 0:SLOT + T], ident)
                last.then_inc(S["v_done"], 1)

            def project_out(s, b, j, wait, first):
                if j == 0:
                    pe.wait_ge(S["ot_loaded"], s * 64 + 64)
                    if b == 0 and not first:
                        pe.wait_ge(S["wo_loaded"], (s - S2) * (16 // NB) + 16)
                if wait:
                    pe.wait_ge(S[wait[0]], wait[1])
                m, i = j // 2, j % 2
                product(proj[j % 2][:, 0:HALF], [(wo[:, c, m * P:(m + 1) * P], OT[:, c, half(i)]) for c in range(KC)])\
                    .then_inc(S["out_done"], 1)

            def maxima(s, b, p):
                if p == 0:
                    pe.wait_ge(S["q_free"], s * HG + HG)
                    pe.wait_ge(S["k_prep"], s * HG + HG)
                    if isinstance(s, int) and s == 0:
                        pe.wait_ge(S["tiles_ready"], NREADY)
                for u in range(2):
                    if not (isinstance(s, int) and s == 0 and p == 0):
                        pe.wait_ge(S["max_ready"], s * 16 + 2 * p - 1 + u)
                    for k in range(2):
                        g = 2 * u + k
                        last = mm(maxb[u][:, k * HT:(k + 1) * HT], QP[:, b % 2, g, p, :], KH[:, b % 2, g, p, :], start=True, stop=True)
                    last.then_inc(S["max_mm"], 1)

            def scores(s, b, p):
                pe.wait_ge(S["maxdiag_ready"], s * PAIRS + p + 1)
                for u in range(2):
                    if not (isinstance(s, int) and s == 0 and p == 0):
                        pe.wait_ge(S["exp_done"], s * 16 + 2 * p - 1 + u)
                    mm(scb[u][:, 0:2 * HT], same_image[:], maxdiag[:, p % 4, u * 8:(u + 1) * 8, :].rearrange("p h t -> p (h t)"),
                       start=True, stop=False)
                    for k in range(2):
                        g = 2 * u + k
                        last = mm(scb[u][:, k * HT:(k + 1) * HT], KP[:, b % 2, g, p, :], QH[:, b % 2, g, p, :], start=False, stop=k == 1)
                    last.then_inc(S["score_done"], 1)

            def values(s, p):
                pe.wait_ge(S["exp_done"], s * 16 + 2 * p + 2)
                pe.wait_ge(S["v_free"], s * PAIRS + p + 1)
                if not (isinstance(s, int) and s == 0 and p < 2):
                    pe.wait_ge(S["o_ready"], s * PAIRS + p - 1)
                o = valb[p % 2]
                for hh in range(HH):
                    for g in range(HG):
                        n = g * HH + hh
                        mm(o[g * 32:(g + 1) * 32, hh * T:(hh + 1) * T],
                           VP[:, p, n].rearrange("k d i -> k (d i)"), probs[:, p % 2, n, :], start=True, stop=True)
                for g in range(HG):
                    last = mm(o[g * 32:(g + 1) * 32, HT:2 * HT], const("ones_pair"),
                              probs[:, p % 2, g * HH:(g + 1) * HH, :].rearrange("p h t -> p (h t)"), start=True, stop=True)
                last.then_inc(S["pv_done"], 1)

            def attend(s, b, follows, nxt, rope, out_prev):
                n, nb = s + 1, nxt

                def outputs(j, *waits):
                    if nxt is None:
                        waits = (("v_free", s * PAIRS + 7), ("v_free", s * PAIRS + 8)) if j == 0 else \
                            (("out_added", (s - 1) * 4 + 1), ("out_added", (s - 1) * 4 + 2))
                    for k in range(2):
                        project_out(s - 1, (b - 1) % NB, j + k, waits[k], rope)

                if not follows:
                    maxima(s, b, 0)
                    maxima(s, b, 1)
                for p in range(PAIRS):
                    if p + 2 < PAIRS:
                        maxima(s, b, p + 2)
                    elif nxt is not None:
                        maxima(n, nb, p + 2 - PAIRS)
                    scores(s, b, p)
                    if nxt is not None and rope and 1 <= p <= HG:
                        rotate(nb, p - 1)
                    if p == 0:
                        turn_v(s, 6, ("v_free", s * PAIRS + 5))
                    if nxt is not None and p == 5:
                        turn_v(n, 0, None)
                        turn_v(n, 1, None)
                    if out_prev and p == 6:
                        outputs(0, ("v_free", n * PAIRS + 3), ("v_free", n * PAIRS + 4))
                    if out_prev and p == 7:
                        outputs(2, ("vt_ready", n * 4 + 4), None)
                    if p:
                        values(s, p - 1)
                    elif follows:
                        values(s - 1, PAIRS - 1)
                    if p == 0:
                        turn_v(s, 7, ("v_free", s * PAIRS + 6))
                    if nxt is not None and p < HG:
                        project_qk(n, nb, p, rope, (("v_free", s * PAIRS + 7), ("v_free", s * PAIRS + 8)) if p == 0 else
                                   qk_free(n, p - 1, rope))
                    if nxt is not None and p == 4:
                        project_v(n, nb, 0, rope, qk_free(n, HG - 1, rope))
                    if nxt is not None and p == 5:
                        turn_v(n, 2, ("v_free", n * PAIRS + 1))
                        turn_v(n, 3, ("v_free", n * PAIRS + 2))
                    if nxt is not None and p == 6:
                        project_v(n, nb, 1, rope, [("out_added", (s - 1) * 4 + 1 + m) if out_prev else ("v_free", n * PAIRS + 3 + m)
                                                   for m in range(KC)])
                    if nxt is not None and p == 7:
                        turn_v(n, 4, ("out_added", (s - 1) * 4 + 3) if out_prev else None)
                        turn_v(n, 5, ("out_added", (s - 1) * 4 + 4) if out_prev else None)

            for g in range(HG):
                project_qk(0, 0, g, True, qk_free(0, g - 1, True) if g else (None, None))
                if g in (0, 3):
                    project_v(0, 0, g // 3, True, (("v_free", 3), ("v_free", 4)) if g else (("obias_made", 1), None), maxb)
                else:
                    for p in (2 * g - 2, 2 * g - 1):
                        turn_v(0, p, ("v_free", p - 1) if p > 1 else None, maxb)
                rotate(0, g)
            turn_v(0, 4, None, maxb)
            turn_v(0, 5, None, maxb)
            pe.wait_ge(S["v_free"], 6)
            for b in range(NB):
                attend(b, b, b > 0, b + 1 if b < NB - 1 else None, True, b > 0)
            values(NB - 1, PAIRS - 1)

            for k in range(NU + 7):
                if k == 3:
                    s = NB - 1
                    for j in range(4):
                        project_out(s, s, j, ("out_added", (s - 1) * 4 + 3 + j) if j < 2 else ("out_added", s * 4 + j - 1), True)
                if k < NU:
                    mean(1, k)
                if 0 <= k - 1 < NU:
                    variance(1, k - 1)
                if 0 <= k - 2 < NU:
                    replicate(1, k - 2)
                if 0 <= k - 3 < NU:
                    u = k - 3
                    b, i = u // 2, u % 2
                    pe.wait_ge(S["normed"], (NU + u + 1) * 2)
                    if u >= 2:
                        pe.wait_ge(S["rcentered"], u - 1)
                    else:
                        pe.wait_ge(S["out_added"], 4 * NB)
                    product(bank[i][:, 0:HALF], [(rw1[:, c, :], xn[:, b, c, half(i)]) for c in range(KC)]).then_inc(S["r_done"], 1)
                if 0 <= k - 4 < NU:
                    u = k - 4
                    pe.wait_ge(S["r_ready"], u + 1)
                    mm(bank[u % 2][:, 0:HALF], const("mean_r"), r[:, half(u)], start=True, stop=True).then_inc(S["rmean_done"], 1)
                if 0 <= k - 5 < NU:
                    u = k - 5
                    pe.wait_ge(S["rsquared"], u + 1)
                    if u >= 2:
                        pe.wait_ge(S["r_normed"], u - 1)
                    variance_of(bank[2 + u % 2], const("mean_r"), [rsq[:, half(u)]]).then_inc(S["rvar_done"], 1)
                if 0 <= k - 6 < NU:
                    u = k - 6
                    pe.wait_ge(S["rrstd"], u + 1)
                    spread(bank[2 + u % 2], rstd[:, 2 + u % 2]).then_inc(S["rrep_done"], 1)
                if 0 <= k - 7 < NU:
                    u = k - 7
                    pe.wait_ge(S["r_relu"], u + 1)
                    for t in range(3 * u, 3 * u + 3):
                        last = mm(bank[4][0:RT, t * NE:(t + 1) * NE], r[:, t * RT:(t + 1) * RT], rw2[:], start=True, stop=True)
            last.then_inc(S["logit_done"], 1)

            def some_biases(n0):
                for n in range(n0, n0 + 4):
                    b, m, i = n // 4, n // 2 % 2, n % 2
                    if n >= 4:
                        pe.wait_ge(S["gobias_added"], n - 3)
                    mm(bank[4 + n % 4][:, 0:HALF], obias[:, m * P:(m + 1) * P], gatesT[b // 2][:, half(2 * (b % 2) + i)],
                       start=True, stop=True).then_inc(S["gobias_done"], 1)

            project_qk(S2, 0, 0, False, (("rcentered", NU), None))
            for p in range(6):
                if p % 4 == 0:
                    project_v(S2, 0, p // 4, False, (("v_free", S2 * PAIRS + 3), ("v_free", S2 * PAIRS + 4)) if p else
                              (("r_normed", NU), None), maxb)
                turn_v(S2, p, ("v_free", S2 * PAIRS + p - 1) if p in (2, 3) else None, maxb)
            pe.wait_ge(S["gates_ready"], 1)
            for u in range(NU):
                if u >= 2:
                    pe.wait_ge(S["gtr_copied"], u - 1)
                for t in range(3):
                    last = nc.tensor.transpose(bank[6 + u % 2][0:NE, t * RT:(t + 1) * RT], gates[:, u * 3 + t, :], ident[0:RT, 0:RT])
                last.then_inc(S["gtr_done"], 1)
            for g in range(1, HG):
                project_qk(S2, 0, g, False, qk_free(S2, g - 1, False))
                if g == 1:
                    pe.wait_ge(S["gtr_copied"], NU)
                    pe.wait_ge(S["obias_made"], 1)
                some_biases((g - 1) * 4)
            some_biases(12)
            pe.wait_ge(S["gobias_added"], 4 * NB)
            pe.wait_ge(S["v_free"], S2 * PAIRS + 6)

            def expert(e, first, last_one):
                for b in range(NB):
                    s = step(e, b)
                    nxt = (b + 1) % NB if not (last_one and b == NB - 1) else None
                    attend(s, b, not (first and b == 0), nxt, False, not (first and b == 0))

            expert(0, True, False)
            with pe.Fori(1, NE - 1) as e:
                expert(e, False, False)
            expert(NE - 1, False, True)
            s = step(NE - 1, NB - 1)
            values(s, PAIRS - 1)
            for j in range(4):
                project_out(s, NB - 1, j, ("out_added", (s - 1) * 4 + 3 + j) if j < 2 else ("out_added", s * 4 + j - 1), False)

        @block.scalar
        def _(act):
            act_f = nc.scalar.activation
            hmask = const("hmask")

            act.wait_ge(S["small_loaded"], NSMALL * 16)

            def square(n, u):
                b, i, w = u // 2, u % 2, n * NU + u
                act.wait_ge(S["centered"], (w + 1) * 2)
                if w >= 2:
                    act.wait_ge(S["var_done"], w - 1)
                act_f(sq[:, :, half(i)], xn[:, b, :, half(i)], ACT.Square).then_inc(S["squared"], 1)

            def root(n, u):
                i, w = u % 2, n * NU + u
                act.wait_ge(S["var_done"], w + 1)
                if w >= 2:
                    act.wait_ge(S["rstd_ready"], w - 1)
                act_f(std[:, i], bank[6 + i][:, 0:NQ], ACT.Sqrt, bias=const("eps"), scale=1.0).then_inc(S["std_ready"], 1)

            for k in range(NU + 2):
                if k < NU:
                    b, i = k // 2, k % 2
                    for m in range(2):
                        act.wait_ge(S["patch_done"], k * 2 + m + 1)
                        act_f(h[:, b, m, half(i)], bank[i * 2 + m][:, 0:HALF], ACT.Identity, bias=tokb[:, m:m + 1], scale=1.0)\
                            .then_inc(S["h_ready"], 1)
                if 0 <= k - 1 < NU:
                    square(0, k - 1)
                if 0 <= k - 2 < NU:
                    root(0, k - 2)

            def keep_raw(b, g):
                for t, done in enumerate(("q_done", "k_done")):
                    n = b * HG + g
                    act.wait_ge(S[done], n + 1)
                    if n:
                        act.wait_ge(S["rope_a_made"], 2 * n + t - 1)
                    act_f(raw[t], proj[t][:, 0:HALF], ACT.Copy).then_inc(S["raw_ready"], 1)

            def prepare_q(s, b, g, rope):
                src = by_token(rope_q if rope else proj[0][:, 0:HALF])
                bias = bias_none if rope else bias_cur
                if rope:
                    act.wait_ge(S["rope_q_ready"], b * HG + g + 1)
                else:
                    act.wait_ge(S["q_done"], s * HG + g + 1)
                for hh in range(HH):
                    act_f(QH[:, b % 2, g, :, hh * T:(hh + 1) * T], src, ACT.Identity,
                          bias=bias[:, g * HH + hh:g * HH + hh + 1], scale=hmask[:, hh:hh + 1])
                for i in range(2):
                    lo, hi = i * 64, (i + 1) * 64
                    last = act_f(QP[lo:hi, b % 2, g, :, i * SLOT:i * SLOT + T], src[lo:hi], ACT.Identity,
                                 bias=bias[lo:hi, 16 + g:17 + g], scale=1.0)
                last.then_inc(S["q_free"], 1)

            def keep_vt(s, a, banks=proj):
                for m in range(KC):
                    act.wait_ge(S["vt_done"], s * 4 + 2 * a + m + 1)
                    act_f(VT[:, m].rearrange("p n (i t) -> p i n t", i=2)[:, :, :, 0:T],
                          banks[m][:, 0:HALF].rearrange("p (i n t) -> p i n t", i=2, t=T), ACT.Copy).then_inc(S["vt_ready"], 1)

            def copy_v(s, p, banks=proj):
                act.wait_ge(S["v_done"], s * PAIRS + p + 1)
                for i in range(2):
                    rows_ = slice(i * SLOT, i * SLOT + T)
                    last = act_f(VP[rows_, p, :, :, i], banks[p % 2][rows_, 0:D].rearrange("k (n d) -> k n d", d=HD), ACT.Copy)
                last.then_inc(S["v_free"], 1)

            def exps(s, p):
                for u in range(2):
                    act.wait_ge(S["score_done"], s * 16 + 2 * p + u + 1)
                    if u == 0 and not (isinstance(s, int) and s == 0 and p < 2):
                        act.wait_ge(S["pv_done"], s * PAIRS + p - 1)
                    act_f(probs[:, p % 2, u * 8:(u + 1) * 8, :], scb[u][:, 0:2 * HT].rearrange("p (h t) -> p h t", t=T),
                          ACT.Exp, scale=HD ** -0.5).then_inc(S["exp_done"], 1)

            def attend(s, b, nxt, rope=False):
                for p in range(PAIRS):
                    exps(s, p)
                    if p == 0:
                        copy_v(s, 6)
                        copy_v(s, 7)
                    if nxt is not None and rope:
                        if 1 <= p <= HG:
                            prepare_q(s + 1, nxt, p - 1, True)
                        if p < HG:
                            keep_raw(nxt, p)
                    elif nxt is not None and p < HG:
                        if p == 0 and nxt == 0:
                            act.wait_ge(S["bias_ready"], (s + 1 - S2) // NB + 1 if isinstance(s, int) else bias_count[0])
                        prepare_q(s + 1, nxt, p, False)
                    if nxt is not None and p in (4, 6):
                        keep_vt(s + 1, p // 2 - 2)
                    if nxt is not None and p in (5, 7):
                        for q in (range(4) if p == 5 else (4, 5)):
                            copy_v(s + 1, q)

            bias_count = [None]
            act.wait_ge(S["tiles_ready"], NREADY)
            for g in range(HG):
                keep_raw(0, g)
                if g in (0, 3):
                    keep_vt(0, g // 3, maxb)
                else:
                    copy_v(0, 2 * g - 2, maxb)
                    copy_v(0, 2 * g - 1, maxb)
                prepare_q(0, 0, g, True)
            copy_v(0, 4, maxb)
            copy_v(0, 5, maxb)
            for b in range(NB):
                attend(b, b, b + 1 if b < NB - 1 else None, True)

            for k in range(NU + 7):
                if k < NU:
                    square(1, k)
                if 0 <= k - 1 < NU:
                    root(1, k - 1)
                if 0 <= k - 3 < NU:
                    u = k - 3
                    act.wait_ge(S["r_done"], u + 1)
                    act_f(r[:, half(u)], bank[u % 2][:, 0:HALF], ACT.Identity, bias=rvec[:, 0:1], scale=1.0).then_inc(S["r_ready"], 1)
                if 0 <= k - 4 < NU:
                    u = k - 4
                    act.wait_ge(S["rcentered"], u + 1)
                    act_f(rsq[:, half(u)], r[:, half(u)], ACT.Square).then_inc(S["rsquared"], 1)
                if 0 <= k - 5 < NU:
                    u = k - 5
                    act.wait_ge(S["rvar_done"], u + 1)
                    if u >= 2:
                        act.wait_ge(S["rrstd"], u - 1)
                    act_f(std[:, 2 + u % 2], bank[2 + u % 2][:, 0:NQ], ACT.Sqrt, bias=const("eps"), scale=1.0).then_inc(S["rstd_done"], 1)
                if 0 <= k - 6 < NU:
                    u = k - 6
                    act.wait_ge(S["r_normed"], u + 1)
                    act_f(r[:, half(u)], r[:, half(u)], ACT.Relu, bias=rvec[:, 2:3], scale=rvec[:, 1:2]).then_inc(S["r_relu"], 1)
            act.wait_ge(S["gstep"], 3)
            act_f(lg[:, 1], lg[:, 0], ACT.Exp).then_inc(S["gexp"], 1)

            act.wait_ge(S["bias_ready"], 1)
            prepare_q(S2, 0, 0, False)
            for p in range(6):
                if p % 4 == 0:
                    keep_vt(S2, p // 4, maxb)
                copy_v(S2, p, maxb)
            for g in range(1, HG):
                prepare_q(S2, 0, g, False)

            def expert(e, last_one):
                bias_count[0] = e + 2
                for b in range(NB):
                    attend(step(e, b), b, (b + 1) % NB if not (last_one and b == NB - 1) else None)

            expert(0, False)
            with act.Fori(1, NE - 1) as e:
                expert(e, False)
            expert(NE - 1, True)

        @block.vector
        def _(dve):
            v = nc.vector
            hmask = const("hmask")

            v.memset(bias_none[:], 0.0).then_inc(S["tiles_ready"], 1)
            v.memset(vb_diag[:], 0.0).then_inc(S["vb_zeroed"], 1)
            dve.wait_ge(S["small_loaded"], NSMALL * 16)
            dve.wait_ge(S["vb_zeroed"], 1)
            v.tensor_copy(vb_diag[:].rearrange("p c e f -> p c (e f)")[:, :, 0:NE * NE:NE + 1], vbT[:]).then_inc(S["vb_ready"], 1)
            v.tensor_copy(same_image[:], const("same_image")).then_inc(S["tiles_ready"], 1)
            for g in range(HG):
                for hh in range(HH):
                    last = v.tensor_scalar(bias_all[:, :, g * HH + hh], bias_all[:, :, 16 + g], hmask[:, hh:hh + 1], None, ALU.mult)
            last.then_inc(S["bias_masked"], 1)
            def center(n, u):
                b, i, w = u // 2, u % 2, n * NU + u
                dve.wait_ge(S["mean_done"], w + 1)
                for c in range(KC):
                    v.tensor_tensor(xn[:, b, c, half(i)], h[:, b, c, half(i)], bank[4 + i][:, 0:HALF],
                                    ALU.subtract).then_inc(S["centered"], 1)

            def invert(n, u):
                i, w = u % 2, n * NU + u
                dve.wait_ge(S["std_ready"], w + 1)
                if w >= 2:
                    dve.wait_ge(S["rep_done"], w - 1)
                v.reciprocal(rstd[:, i], std[:, i]).then_inc(S["rstd_ready"], 1)

            def scale(n, u):
                b, i, w = u // 2, u % 2, n * NU + u
                dve.wait_ge(S["rep_done"], w + 1)
                for c in range(KC):
                    xs = xn[:, b, c, half(i)]
                    v.tensor_tensor(xs, xs, bank[6 + i][:, 0:HALF], ALU.mult).then_inc(S["normed"], 1)

            for k in range(1, NU + 3):
                if 0 <= k - 1 < NU:
                    center(0, k - 1)
                if 0 <= k - 2 < NU:
                    invert(0, k - 2)
                if 0 <= k - 3 < NU:
                    scale(0, k - 3)
            dve.wait_ge(S["obias_done"], 1)
            v.tensor_tensor(obias[:], bank[3][0:NE, 0:D], ob_nat[:], ALU.add).then_inc(S["obias_made"], 1)

            def rope_sum(s, b, g):
                sin = const("sin").unsqueeze(1).to_broadcast([P, PAIRS, T])
                n = s * HG + g
                for t, (dst, ready, free) in enumerate(((rope_q, "rope_q_ready", "q_free"), (rope_k, "rope_k_ready", "k_free"))):
                    if n:
                        dve.wait_ge(S[ready], n)
                    dve.wait_ge(S["rot_done"], 2 * n + t + 1)
                    v.tensor_tensor(by_token(rope_b[:, t]), by_token(proj[t][:, 0:HALF]), sin, ALU.mult).then_inc(S["rope_b_made"], 1)
                    dve.wait_ge(S["rope_b_made"], 2 * n + t + 1)
                    dve.wait_ge(S["rope_a_made"], 2 * n + t + 1)
                    if n:
                        dve.wait_ge(S[free], n)
                    v.tensor_tensor(dst, rope_a[:, t], rope_b[:, t], ALU.add).then_inc(S[ready], 1)
                dve.wait_ge(S["rope_k_ready"], n + 1)

            def prepare_k(s, b, g, rope):
                src = by_token(rope_k if rope else proj[1][:, 0:HALF])
                bias = bias_none if rope else bias_cur
                if not rope:
                    dve.wait_ge(S["k_done"], s * HG + g + 1)
                for i in range(2):
                    lo, hi = i * 64, (i + 1) * 64
                    v.tensor_scalar(KP[lo:hi, b % 2, g, :, i * SLOT:i * SLOT + T], src[lo:hi], bias[lo:hi, 20 + g:21 + g], None, ALU.add)
                if not (isinstance(s, int) and s == 0 and g == 0):
                    dve.wait_ge(S["k_prep"], s * HG + g)
                v.tensor_scalar(by_token(Kb[:]), src, bias[:, 20 + g:21 + g], None, ALU.add).then_inc(S["k_free"], 1)
                dve.wait_ge(S["k_free"], s * HG + g + 1)
                for hh in range(HH):
                    last = v.tensor_scalar(KH[:, b % 2, g, :, hh * T:(hh + 1) * T], by_token(Kb[:]), hmask[:, hh:hh + 1], None, ALU.mult)
                last.then_inc(S["k_prep"], 1)

            def add_out(s, b, j, bias):
                m, i = j // 2, j % 2
                dve.wait_ge(S["out_done"], s * 4 + j + 1)
                hs = h[:, b, m, half(i)]
                if bias is None:
                    last = v.tensor_tensor(hs, proj[j % 2][:, 0:HALF], hs, ALU.add)
                else:
                    last = v.scalar_tensor_tensor(out=hs, in0=proj[j % 2][:, 0:HALF], scalar=bias[:, m:m + 1], in1=hs,
                                                  op0=ALU.add, op1=ALU.add)
                last.then_inc(S["out_added"], 1)

            def reduce_max(s, p):
                if not (isinstance(s, int) and s == 0 and p < 4):
                    dve.wait_ge(S["maxdiag_ready"], s * PAIRS + p - 3)
                for u in range(2):
                    dve.wait_ge(S["max_mm"], s * 16 + 2 * p + u + 1)
                    v.tensor_reduce(rowmax[:, p % 4, u * 8:(u + 1) * 8], maxb[u][:, 0:2 * HT].rearrange("p (h t) -> p h t", t=T), AX,
                                    ALU.max).then_inc(S["max_ready"], 1)

            def normalize(s, b, p, gated):
                n = s * PAIRS + p
                dve.wait_ge(S["pv_done"], n + 1)
                if not (isinstance(s, int) and s == 0 and p < 2):
                    dve.wait_ge(S["o_ready"], n - 1)
                o = valb[p % 2]
                v.reciprocal(rsum[:, p % 2], o[:, HT:2 * HT].rearrange("p (h t) -> p h t", t=T)).then_inc(S["rsum_ready"], 1)
                if p == 0 and not (isinstance(s, int) and s == 0):
                    dve.wait_ge(S["ot_loaded"], s * 64)
                dve.wait_ge(S["rsum_ready"], n + 1)
                factor = rsum
                if gated:
                    if p == 0:
                        dve.wait_ge(S[f"gate_loaded{b % 2}"], (s - b - S2) * 16 + b // 2 * 32 + 32)
                    v.tensor_tensor(scale_o[:, p % 2], rsum[:, p % 2], gate_rep[:, b % 2, p:p + 1, :].to_broadcast([P, HH, T]),
                                    ALU.mult).then_inc(S["scale_ready"], 1)
                    dve.wait_ge(S["scale_ready"], n - S2 * PAIRS + 1)
                    factor = scale_o
                v.tensor_tensor(ON[:, :, p, :], o[:, 0:HT].rearrange("p (h t) -> p h t", t=T), factor[:, p % 2],
                                ALU.mult).then_inc(S["o_ready"], 1)

            def attend(s, b, follows, nxt, rope, out_prev):
                def outputs(j):
                    for k in range(2):
                        add_out(s - 1, (b - 1) % NB, j + k, bout if rope else None)

                if not follows:
                    reduce_max(s, 0)
                    reduce_max(s, 1)
                for p in range(PAIRS):
                    if p + 2 < PAIRS:
                        reduce_max(s, p + 2)
                    elif nxt is not None:
                        reduce_max(s + 1, p + 2 - PAIRS)
                    if out_prev and p == 7:
                        outputs(2)
                    if nxt is not None and rope and 1 <= p <= HG:
                        rope_sum(s + 1, nxt, p - 1)
                    if p:
                        normalize(s, b, p - 1, not rope)
                    elif follows:
                        normalize(s - 1, (b - 1) % NB, PAIRS - 1, not rope)
                    if nxt is not None and rope and 1 <= p <= HG:
                        prepare_k(s + 1, nxt, p - 1, True)
                    if nxt is not None and p < HG and not rope:
                        if p == 0 and nxt == 0:
                            dve.wait_ge(S["bias_ready"], bias_count[0])
                        prepare_k(s + 1, nxt, p, False)
                    if out_prev and p == 5:
                        outputs(0)

            bias_count = [None]
            dve.wait_ge(S["tiles_ready"], NREADY)
            for g in range(HG):
                rope_sum(0, 0, g)
                prepare_k(0, 0, g, True)
            for b in range(NB):
                attend(b, b, b > 0, b + 1 if b < NB - 1 else None, True, b > 0)
            normalize(NB - 1, NB - 1, PAIRS - 1, False)

            for k in range(NU + 7):
                if k == 3:
                    for j in range(4):
                        add_out(NB - 1, NB - 1, j, bout)
                if k < NU:
                    center(1, k)
                if 0 <= k - 1 < NU:
                    invert(1, k - 1)
                if 0 <= k - 2 < NU:
                    scale(1, k - 2)
                if 0 <= k - 4 < NU:
                    u = k - 4
                    dve.wait_ge(S["rmean_done"], u + 1)
                    v.tensor_tensor(r[:, half(u)], r[:, half(u)], bank[u % 2][:, 0:HALF], ALU.subtract).then_inc(S["rcentered"], 1)
                if 0 <= k - 5 < NU:
                    u = k - 5
                    dve.wait_ge(S["rstd_done"], u + 1)
                    if u >= 2:
                        dve.wait_ge(S["rrep_done"], u - 1)
                    v.reciprocal(rstd[:, 2 + u % 2], std[:, 2 + u % 2]).then_inc(S["rrstd"], 1)
                if 0 <= k - 6 < NU:
                    u = k - 6
                    dve.wait_ge(S["rrep_done"], u + 1)
                    v.tensor_tensor(r[:, half(u)], r[:, half(u)], bank[2 + u % 2][:, 0:HALF], ALU.mult).then_inc(S["r_normed"], 1)

            done = [0]

            def then(ins):
                done[0] += 1
                ins.then_inc(S["gstep"], 1)
                dve.wait_ge(S["gstep"], done[0])

            wide = lambda a: a.unsqueeze(2).to_broadcast([RT, NT, NE])
            dve.wait_ge(S["logit_done"], 1)
            logits = bank[4][0:RT, 0:NT * NE].rearrange("p (t e) -> p t e", e=NE)
            then(v.tensor_tensor(lg[:, 1], logits, rb2_rep[:].unsqueeze(1).to_broadcast([RT, NT, NE]), ALU.add))
            then(v.tensor_reduce(rs[:, 0], lg[:, 1], AX, ALU.max))
            then(v.tensor_tensor(lg[:, 0], lg[:, 1], wide(rs[:, 0]), ALU.subtract))
            dve.wait_ge(S["gexp"], 1)
            then(v.tensor_reduce(rs[:, 1], lg[:, 1], AX, ALU.add))
            then(v.reciprocal(rs[:, 2], rs[:, 1]))
            then(v.tensor_tensor(lg[:, 2], lg[:, 1], wide(rs[:, 2]), ALU.mult))
            for t in range(NT):
                last = v.max(top[:, t, :], lg[:, 2, t, :])
            then(last)
            for t in range(NT):
                last = v.max_index(topi[:, t, :], top[:, t, :], lg[:, 2, t, :])
            then(last)
            then(v.tensor_copy(topf[:], topi[:]))
            then(v.tensor_tensor(rs[:, 3], top[:, :, 0], top[:, :, 1], ALU.add))
            then(v.reciprocal(rs[:, 0], rs[:, 3]))
            iota = const("iota", RT).unsqueeze(1).to_broadcast([RT, NT, NE])
            for k in range(2):
                then(v.tensor_tensor(gsel[:, k], iota, wide(topf[:, :, k]), ALU.is_equal))
                then(v.tensor_tensor(gsel[:, k], gsel[:, k], wide(top[:, :, k]), ALU.mult))
            then(v.tensor_tensor(lg[:, 3], gsel[:, 0], gsel[:, 1], ALU.add))
            v.tensor_tensor(gates[:], lg[:, 3], wide(rs[:, 0]), ALU.mult).then_inc(S["gates_ready"], 1)
            dve.wait_ge(S["bias_ready"], 1)
            prepare_k(S2, 0, 0, False)
            for u in range(NU):
                dve.wait_ge(S["gtr_done"], u + 1)
                v.tensor_copy(gatesT[u // 4][:, half(u % 4)], bank[6 + u % 2][0:NE, 0:HALF]).then_inc(S["gtr_copied"], 1)
            for g in range(1, HG + 1):
                if g < HG:
                    prepare_k(S2, 0, g, False)
                for n in range(4 * g - 4, 4 * g):
                    b, m, i = n // 4, n // 2 % 2, n % 2
                    dve.wait_ge(S["gobias_done"], n + 1)
                    hs = h[:, b, m, half(i)]
                    v.tensor_tensor(hs, bank[4 + n % 4][:, 0:HALF], hs, ALU.add).then_inc(S["gobias_added"], 1)

            def expert(e, first, last_one):
                bias_count[0] = e + 2
                for b in range(NB):
                    nxt = (b + 1) % NB if not (last_one and b == NB - 1) else None
                    attend(step(e, b), b, not (first and b == 0), nxt, False, not (first and b == 0))

            expert(0, True, False)
            with dve.Fori(1, NE - 1) as e:
                expert(e, False, False)
            expert(NE - 1, False, True)
            s = step(NE - 1, NB - 1)
            normalize(s, NB - 1, PAIRS - 1, True)
            for j in range(4):
                add_out(s, NB - 1, j, None)

        @block.gpsimd
        def _(pool):
            g_ = nc.gpsimd
            g_.memset(QP[:, 0].bitcast(F32), 0.0).then_inc(S["tiles_ready"], 1)
            g_.memset(QP[:, 1].bitcast(F32), 0.0).then_inc(S["tiles_ready"], 1)
            g_.memset(VT[:], 0.0).then_inc(S["tiles_ready"], 1)
            g_.memset(VP[:], 0.0).then_inc(S["tiles_ready"], 1)
            pool.wait_ge(S["small_loaded"], NSMALL * 16)
            pool.wait_ge(S["obias_done"], 1)
            g_.memset(KP[:, 0], 0.0).then_inc(S["tiles_ready"], 1)
            pool.wait_ge(S["patch_done"], 4 * NB)
            g_.memset(KP[:, 1], 0.0).then_inc(S["tiles_ready"], 1)

            def diagonal(s, p):
                pool.wait_ge(S["max_ready"], s * 16 + 2 * p + 2)
                if not (isinstance(s, int) and s == 0 and p < 4):
                    pool.wait_ge(S["score_done"], s * 16 + 2 * (p - 3))
                g_.tensor_tensor(maxdiag[:, p % 4], rowmax[:, p % 4].unsqueeze(2).to_broadcast([P, HEADS, T]),
                                 const("negdiag").unsqueeze(1).to_broadcast([P, HEADS, T]), ALU.mult).then_inc(S["maxdiag_ready"], 1)

            def load_bias(e):
                src = bias_all[:, e] if isinstance(e, int) else bias_all[:, bass.ds(e, 1), :].rearrange("p o n -> p (o n)")
                g_.tensor_copy(bias_cur[:], src).then_inc(S["bias_ready"], 1)

            pool.wait_ge(S["bias_masked"], 1)
            load_bias(0)
            def rope_cos(b, g):
                n = b * HG + g
                cos = const("cos").unsqueeze(1).to_broadcast([P, PAIRS, T])
                for t, ready in enumerate(("rope_q_ready", "rope_k_ready")):
                    pool.wait_ge(S["raw_ready"], 2 * n + t + 1)
                    if n:
                        pool.wait_ge(S[ready], n)
                    g_.tensor_tensor(by_token(rope_a[:, t]), by_token(raw[t]), cos, ALU.mult).then_inc(S["rope_a_made"], 1)

            for g in range(HG):
                rope_cos(0, g)
            for b in range(NB):
                for p in range(PAIRS):
                    diagonal(b, p)
                    if b < NB - 1 and 2 <= p < 2 + HG:
                        rope_cos(b + 1, p - 2)

            def expert(e, last_one):
                for b in range(NB):
                    s = step(e, b)
                    for p in range(PAIRS):
                        diagonal(s, p)
                        if b == NB - 2 and p == 6 and not last_one:
                            pool.wait_ge(S["q_free"], (s + 1) * HG + HG)
                            pool.wait_ge(S["k_free"], (s + 1) * HG + HG)
                            load_bias(e + 1)

            expert(0, False)
            with pool.Fori(1, NE - 1) as e:
                expert(e, False)
            expert(NE - 1, True)


def rows(a, n=P):
    return a.reshape(-1, n, *a.shape[1:]).swapaxes(0, 1)


def kernel(x, L0_tok_W, L0_tok_b, L0_attn_w_qkv, L0_attn_w_out, L0_attn_b_out, L0_ffn_rW1, L0_ffn_rb1, L0_ffn_ln_g,
           L0_ffn_ln_b, L0_ffn_rW2, L0_ffn_rb2, L0_ffn_qW, L0_ffn_qb, L0_ffn_kW, L0_ffn_kb, L0_ffn_vW, L0_ffn_vb,
           L0_ffn_oW, L0_ffn_ob):
    import concourse.bacc as _bacc
    from concourse.bass_utils import run_bass_kernel_spmd as _run

    pixels = np.asarray(x).reshape(NB, BATCH, CHANNELS, GRID, PATCH, GRID, PATCH).transpose(0, 2, 4, 6, 1, 3, 5)
    pixels = pixels.reshape(NB, FC, P, TOK).swapaxes(1, 2)

    def heads_rows(w):
        return np.asarray(w).reshape(HG, 2, 2, HD, -1).transpose(2, 0, 3, 1, 4).reshape(P, KC, -1)

    qkv = np.asarray(L0_attn_w_qkv)
    experts = [np.stack([rows(np.asarray(w)[e].T) for w in (L0_ffn_qW, L0_ffn_kW, L0_ffn_vW)]
                        + [heads_rows(np.asarray(L0_ffn_oW)[e].T)], axis=1) for e in range(NE)]
    qkb = np.stack([np.asarray(b).reshape(NE, HG, SLOT) for b in (L0_ffn_qb, L0_ffn_kb)], axis=1)
    qkb = np.concatenate([qkb.transpose(3, 0, 1, 2).reshape(SLOT, NE, 2 * HG)] * 2)
    arrays = {
        "pixels": pixels, "tok_W": rows(np.asarray(L0_tok_W).T), "tok_b": rows(np.asarray(L0_tok_b)),
        "w_qkv": rows(qkv), "w_out": heads_rows(L0_attn_w_out), "b_out": rows(np.asarray(L0_attn_b_out)),
        "rW1": rows(np.asarray(L0_ffn_rW1).T), "rvec": np.stack([np.asarray(a) for a in (L0_ffn_rb1, L0_ffn_ln_g, L0_ffn_ln_b)], axis=1),
        "rW2": np.asarray(L0_ffn_rW2).T, "rb2": np.asarray(L0_ffn_rb2)[None], "experts": np.stack(experts), "qk_bias": qkb,
        "v_bias": heads_rows(np.asarray(L0_ffn_vb).T), "oW": np.stack([e[:, 3] for e in experts], axis=1),
        "o_bias": np.asarray(L0_ffn_ob), "table": constants(),
    }
    arrays = {k: np.ascontiguousarray(a) for k, a in arrays.items()}
    nc = _bacc.Bacc("TRN2", target_bir_lowering=False, num_devices=1)
    args = [nc.dram_tensor(f"in_{name}", a.shape, mybir.dt.from_np(a.dtype), kind="ExternalInput").ap()
            for name, a in arrays.items()]
    out = nc.dram_tensor("out_h", (NB, P, KC, TOK), F32, kind="ExternalOutput").ap()
    build(nc, *args, out)
    r = _run(nc, [{f"in_{k}": a for k, a in arrays.items()}], core_ids=[0])
    return r.results[0]["out_h"].transpose(0, 3, 2, 1).reshape(IMAGES, T, D)
```
